# Optimizing a Trainium2 kernel written in Bass

```python
import numpy as np
import jax
import jax.numpy as jnp

def _softmax(x, axis=-1):
    return jax.nn.softmax(x, axis=axis)

def _gelu(x):
    return jax.nn.gelu(x, approximate=True)

def _silu(x):
    return jax.nn.silu(x)

def _sigmoid(x):
    return jax.nn.sigmoid(x)

def _layernorm(x, axis=-1, eps=1e-05):
    m = jnp.mean(x, axis=axis, keepdims=True)
    v = jnp.var(x, axis=axis, keepdims=True)
    return (x - m) / jnp.sqrt(v + eps)

def _scatter_add(tgt, idx, src, axis=0):
    return tgt.at[idx].add(src)

def _segment_sum(src, seg, n):
    return jax.ops.segment_sum(src, seg, n)
kernel_name = 'mk_cond_seq_d2_seqx_r8_0d108c'

def setup_inputs(seed: int=0):
    np.random.seed(seed)
    _w = jnp.asarray

    def _rec_inputs():
        import jax
        import jax.numpy as jnp
        _rk = jax.random.key(seed)
        x = 7.22e-05 + 1 * jax.random.normal(jax.random.fold_in(_rk, 1), (128, 32, 128), jnp.float32)
        _lenS = 32 - jax.random.randint(jax.random.fold_in(_rk, 7), (128,), 0, max(1, 32 // 4) + 1, jnp.int32)
        _lenS2 = 32 - jax.random.randint(jax.random.fold_in(_rk, 8), (128,), 0, max(1, 32 // 4) + 1, jnp.int32)
        cond_2048 = 0.00782532 + 1.00527 * jax.random.normal(jax.random.fold_in(_rk, 11), (128, 256), jnp.float32)
        _validS = jnp.arange(32)[None, :] < _lenS[:, None]
        _validS2 = jnp.arange(32)[None, :] < _lenS2[:, None]
        _causal = jnp.tril(jnp.ones((32, 32), dtype=bool))
        mask_BxSx1_fk1 = jnp.where(jnp.ones((128, 32, 1), dtype=bool), 1.0, 0.0).astype(jnp.float32)
        mask_BxS_ik0 = jnp.where(jnp.broadcast_to(_validS[:, :], (128, 32)), 0, 1).astype(jnp.int32)
        return (x, cond_2048, mask_BxSx1_fk1, mask_BxS_ik0)
    x, cond_2048, mask_BxSx1_fk1, mask_BxS_ik0 = _rec_inputs()

    def _L0_cond_setup():
        import jax, jax.numpy as jnp
        import numpy as np
        B, T, D, H, TE = (4, 256, 128, 8, 256)
        EPS = 1e-05

        def _ln(x, w, b):
            m = jnp.mean(x, axis=-1, keepdims=True)
            v = jnp.mean((x - m) ** 2, axis=-1, keepdims=True)
            return (x - m) * jax.lax.rsqrt(v + EPS) * w + b
        key = jax.random.key(seed)
        ks = jax.random.split(key, 16)
        s = 0.02
        inp = {'x': jax.random.normal(ks[0], (B, T, D), jnp.float32), 'emb': jax.random.normal(ks[1], (B, TE), jnp.float32), 'src_mask': (jax.random.uniform(ks[2], (B, T, 1)) > 0.2).astype(jnp.float32), 'num_head': H, 'ln_w': jnp.ones((D,), jnp.float32), 'ln_b': jnp.zeros((D,), jnp.float32), 'Wq': jax.random.normal(ks[3], (D, D), jnp.float32) * s, 'bq': jnp.zeros((D,), jnp.float32), 'Wk': jax.random.normal(ks[4], (D, D), jnp.float32) * s, 'bk': jnp.zeros((D,), jnp.float32), 'Wv': jax.random.normal(ks[5], (D, D), jnp.float32) * s, 'bv': jnp.zeros((D,), jnp.float32), 'W_emb': jax.random.normal(ks[6], (TE, 2 * D), jnp.float32) * s, 'b_emb': jnp.zeros((2 * D,), jnp.float32), 'ln2_w': jnp.ones((D,), jnp.float32), 'ln2_b': jnp.zeros((D,), jnp.float32), 'W_out': jax.random.normal(ks[7], (D, D), jnp.float32) * s, 'b_out': jnp.zeros((D,), jnp.float32)}
        return inp
    _L0_cond_all = _L0_cond_setup()
    _L0_cond_in = {k: v for k, v in _L0_cond_all.items() if k in ('ln_w', 'ln_b', 'Wq', 'bq', 'Wk', 'bk', 'Wv', 'bv', 'W_emb', 'b_emb', 'ln2_w', 'ln2_b', 'W_out', 'b_out')}
    del _L0_cond_all

    def _L1_cond_setup():
        import jax, jax.numpy as jnp
        import numpy as np
        H = 16
        LN_EPS = 1e-05

        def _layernorm(x, scale, bias):
            mu = jnp.mean(x, axis=-1, keepdims=True)
            var = jnp.var(x, axis=-1, keepdims=True)
            return (x - mu) * jax.lax.rsqrt(var + LN_EPS) * scale + bias
        key = jax.random.key(seed)
        ks = jax.random.split(key, 8)
        B, T, D, E = (4, 512, 128, 256)
        s = 0.02
        return {'x': jax.random.normal(ks[0], (B, T, D), jnp.float32), 'emb': jax.random.normal(ks[1], (B, E), jnp.float32), 'src_mask': jax.random.randint(ks[2], (B, T), 0, 2).astype(jnp.int32), 'norm_scale': jnp.ones((D,), jnp.float32), 'norm_bias': jnp.zeros((D,), jnp.float32), 'Wq': jax.random.normal(ks[3], (D, D), jnp.float32) * s, 'bq': jnp.zeros((D,), jnp.float32), 'Wk': jax.random.normal(ks[4], (D, D), jnp.float32) * s, 'bk': jnp.zeros((D,), jnp.float32), 'Wv': jax.random.normal(ks[5], (D, D), jnp.float32) * s, 'bv': jnp.zeros((D,), jnp.float32), 'film_emb_W': jax.random.normal(ks[6], (E, 2 * D), jnp.float32) * s, 'film_emb_b': jnp.zeros((2 * D,), jnp.float32), 'film_norm_scale': jnp.ones((D,), jnp.float32), 'film_norm_bias': jnp.zeros((D,), jnp.float32), 'film_out_W': jax.random.normal(ks[7], (D, D), jnp.float32) * s, 'film_out_b': jnp.zeros((D,), jnp.float32)}
    _L1_cond_all = _L1_cond_setup()
    _L1_cond_in = {k: v for k, v in _L1_cond_all.items() if k in ('norm_scale', 'norm_bias', 'Wq', 'bq', 'Wk', 'bk', 'Wv', 'bv', 'film_emb_W', 'film_emb_b', 'film_norm_scale', 'film_norm_bias', 'film_out_W', 'film_out_b')}
    del _L1_cond_all
    return {'x': x, 'cond_2048': cond_2048, 'mask_BxSx1_fk1': mask_BxSx1_fk1, 'mask_BxS_ik0': mask_BxS_ik0, 'L0_cond_ln_w': _L0_cond_in['ln_w'], 'L0_cond_ln_b': _L0_cond_in['ln_b'], 'L0_cond_Wq': _L0_cond_in['Wq'], 'L0_cond_bq': _L0_cond_in['bq'], 'L0_cond_Wk': _L0_cond_in['Wk'], 'L0_cond_bk': _L0_cond_in['bk'], 'L0_cond_Wv': _L0_cond_in['Wv'], 'L0_cond_bv': _L0_cond_in['bv'], 'L0_cond_W_emb': _L0_cond_in['W_emb'], 'L0_cond_b_emb': _L0_cond_in['b_emb'], 'L0_cond_ln2_w': _L0_cond_in['ln2_w'], 'L0_cond_ln2_b': _L0_cond_in['ln2_b'], 'L0_cond_W_out': _L0_cond_in['W_out'], 'L0_cond_b_out': _L0_cond_in['b_out'], 'L1_cond_norm_scale': _L1_cond_in['norm_scale'], 'L1_cond_norm_bias': _L1_cond_in['norm_bias'], 'L1_cond_Wq': _L1_cond_in['Wq'], 'L1_cond_bq': _L1_cond_in['bq'], 'L1_cond_Wk': _L1_cond_in['Wk'], 'L1_cond_bk': _L1_cond_in['bk'], 'L1_cond_Wv': _L1_cond_in['Wv'], 'L1_cond_bv': _L1_cond_in['bv'], 'L1_cond_film_emb_W': _L1_cond_in['film_emb_W'], 'L1_cond_film_emb_b': _L1_cond_in['film_emb_b'], 'L1_cond_film_norm_scale': _L1_cond_in['film_norm_scale'], 'L1_cond_film_norm_bias': _L1_cond_in['film_norm_bias'], 'L1_cond_film_out_W': _L1_cond_in['film_out_W'], 'L1_cond_film_out_b': _L1_cond_in['film_out_b']}

def reference(x, cond_2048, mask_BxSx1_fk1, mask_BxS_ik0, L0_cond_ln_w, L0_cond_ln_b, L0_cond_Wq, L0_cond_bq, L0_cond_Wk, L0_cond_bk, L0_cond_Wv, L0_cond_bv, L0_cond_W_emb, L0_cond_b_emb, L0_cond_ln2_w, L0_cond_ln2_b, L0_cond_W_out, L0_cond_b_out, L1_cond_norm_scale, L1_cond_norm_bias, L1_cond_Wq, L1_cond_bq, L1_cond_Wk, L1_cond_bk, L1_cond_Wv, L1_cond_bv, L1_cond_film_emb_W, L1_cond_film_emb_b, L1_cond_film_norm_scale, L1_cond_film_norm_bias, L1_cond_film_out_W, L1_cond_film_out_b):
    import jax
    import jax.numpy as jnp

    def _L0_cond_ref(x, emb, src_mask, num_head, ln_w, ln_b, Wq, bq, Wk, bk, Wv, bv, W_emb, b_emb, ln2_w, ln2_b, W_out, b_out):
        import jax, jax.numpy as jnp
        import numpy as np
        B, T, D, H, TE = (4, 256, 128, 8, 256)
        EPS = 1e-05

        def _ln(x, w, b):
            m = jnp.mean(x, axis=-1, keepdims=True)
            v = jnp.mean((x - m) ** 2, axis=-1, keepdims=True)
            return (x - m) * jax.lax.rsqrt(v + EPS) * w + b
        b, t, d = x.shape
        h = num_head
        dh = d // h
        xn = _ln(x, ln_w, ln_b)
        q = xn @ Wq + bq
        k = xn @ Wk + bk + (1.0 - src_mask) * -1000000.0
        q = jax.nn.softmax(q.reshape(b, t, h, dh), axis=-1)
        k = jax.nn.softmax(k.reshape(b, t, h, dh), axis=1)
        v = ((xn @ Wv + bv) * src_mask).reshape(b, t, h, dh)
        att = jnp.einsum('bnhd,bnhl->bhdl', k, v)
        y = jnp.einsum('bnhd,bhdl->bnhl', q, att).reshape(b, t, d)
        emb_out = (jax.nn.silu(emb) @ W_emb + b_emb)[:, None, :]
        scale, shift = jnp.split(emb_out, 2, axis=2)
        hh = _ln(y, ln2_w, ln2_b) * (1.0 + scale) + shift
        hh = jax.nn.silu(hh) @ W_out + b_out
        return x + hh

    def _L1_cond_ref(x, emb, src_mask, norm_scale, norm_bias, Wq, bq, Wk, bk, Wv, bv, film_emb_W, film_emb_b, film_norm_scale, film_norm_bias, film_out_W, film_out_b):
        import jax, jax.numpy as jnp
        import numpy as np
        H = 16
        LN_EPS = 1e-05

        def _layernorm(x, scale, bias):
            mu = jnp.mean(x, axis=-1, keepdims=True)
            var = jnp.var(x, axis=-1, keepdims=True)
            return (x - mu) * jax.lax.rsqrt(var + LN_EPS) * scale + bias
        B, T, D = x.shape
        dh = D // H
        xn = _layernorm(x, norm_scale, norm_bias)
        q = xn @ Wq + bq
        k = xn @ Wk + bk
        v = xn @ Wv + bv
        mask = (src_mask == 1)[:, :, None]
        k = jnp.where(mask, -jnp.inf, k)
        v = jnp.where(mask, 0.0, v)
        q = q.reshape(B, T, H, dh).transpose(0, 2, 1, 3)
        k = k.reshape(B, T, H, dh).transpose(0, 2, 1, 3)
        v = v.reshape(B, T, H, dh).transpose(0, 2, 1, 3)
        q = jax.nn.softmax(q, axis=-1)
        k = jax.nn.softmax(k, axis=2)
        attn = jnp.einsum('bhse,bhsd->bhed', k, v)
        y = jnp.einsum('bhtd,bhed->bhte', q, attn)
        y = y.transpose(0, 2, 1, 3).reshape(B, T, D)
        emb_out = jax.nn.silu(emb) @ film_emb_W + film_emb_b
        scale, shift = jnp.split(emb_out, 2, axis=-1)
        h = _layernorm(y, film_norm_scale, film_norm_bias) * (1.0 + scale[:, None, :]) + shift[:, None, :]
        h = jax.nn.silu(h) @ film_out_W + film_out_b
        return x + h
    x = _L0_cond_ref(x, cond_2048, mask_BxSx1_fk1, 8, L0_cond_ln_w, L0_cond_ln_b, L0_cond_Wq, L0_cond_bq, L0_cond_Wk, L0_cond_bk, L0_cond_Wv, L0_cond_bv, L0_cond_W_emb, L0_cond_b_emb, L0_cond_ln2_w, L0_cond_ln2_b, L0_cond_W_out, L0_cond_b_out)
    x = _L1_cond_ref(x, cond_2048, mask_BxS_ik0, L1_cond_norm_scale, L1_cond_norm_bias, L1_cond_Wq, L1_cond_bq, L1_cond_Wk, L1_cond_bk, L1_cond_Wv, L1_cond_bv, L1_cond_film_emb_W, L1_cond_film_emb_b, L1_cond_film_norm_scale, L1_cond_film_norm_bias, L1_cond_film_out_W, L1_cond_film_out_b)
    return x

_drawn_inputs = setup_inputs


def setup_inputs(seed=0):
    import zlib

    import numpy as np

    out = dict(_drawn_inputs(seed))
    spreads = {'L0_cond_ln_w': (1.0, 0.6),
     'L0_cond_ln_b': (0.0, 0.334),
     'L0_cond_bq': (0.0, 0.8),
     'L0_cond_bk': (0.0, 2.0),
     'L0_cond_bv': (0.0, 0.1),
     'L0_cond_b_emb': (0.0, 0.306),
     'L0_cond_ln2_w': (1.0, 0.2),
     'L0_cond_ln2_b': (0.0, 0.629),
     'L0_cond_b_out': (0.0, 0.1),
     'L1_cond_norm_scale': (1.0, 0.6),
     'L1_cond_norm_bias': (0.0, 0.403),
     'L1_cond_bq': (0.0, 0.8),
     'L1_cond_bk': (0.0, 2.0),
     'L1_cond_bv': (0.0, 0.1),
     'L1_cond_film_emb_b': (0.0, 0.489),
     'L1_cond_film_norm_scale': (1.0, 0.578),
     'L1_cond_film_norm_bias': (0.0, 0.476),
     'L1_cond_film_out_b': (0.0, 0.1)}
    factors = {'L0_cond_Wq': 8.0, 'L0_cond_Wk': 8.0, 'L1_cond_Wk': 4.307}
    for name, (base, spread) in spreads.items():
        noise = np.random.default_rng([zlib.crc32(name.encode()), seed]).standard_normal(out[name].shape)
        drawn = base * np.exp(spread * noise) if base else spread * noise
        out[name] = jnp.asarray(drawn.astype(out[name].dtype))
    for name, factor in factors.items():
        out[name] = (out[name] * factor).astype(out[name].dtype)
    return out
```

```python
from contextlib import ExitStack

import concourse.bass as bass
from concourse import mybir

F32 = mybir.dt.float32
BF16 = mybir.dt.bfloat16
I32 = mybir.dt.int32
ALU = mybir.AluOpType
ACT = mybir.ActivationFunctionType
X = mybir.AxisListType.X

P = 128
B, T, D = 128, 32, 128
E = 256
EC = E // P
NT = B * T // P
TG = 4
NG = NT // TG
BT = P // T
BG = BT * TG
R = TG * P
Q = 32
NQ = P // Q
HEADS = (8, 16)
EPS = 1e-5
PARTS = 3

LNW, LNB, BK, BSCALE, BSHIFT, LN2W, LN2B = range(7)
NVEC = 7


def build(nc, x, cond, mask_f, mask_i, layers, out):
    ctx = ExitStack()
    with ctx:
        def sb(name, shape, dt=F32):
            return ctx.enter_context(nc.sbuf_tensor(name, shape, dt))

        def both(make, name, *args):
            return [make(f"{name}{n}", *args) for n in range(2)]

        def sem(name):
            return ctx.enter_context(nc.semaphore(name))

        ident = sb("ident", [P, P])
        head_of = [sb(f"head_of{n}", [P, HEADS[n]]) for n in range(2)]
        head_mask = both(sb, "head_mask", [P, Q])
        exponent = sb("exponent", [P, TG])
        ones3 = sb("ones3", [PARTS, P], BF16)
        vectors = sb("vectors", [2 * NVEC, P])
        vcol = sb("vcol", [P, 2 * NVEC])
        w_raw = both(sb, "w_raw", [P, 3 * D])
        w_in = both(sb, "w_in", [P, 3 * D])
        w_emb = both(sb, "w_emb", [P, EC, 2 * D])
        w_out = both(sb, "w_out", [P, D])
        b_rows = both(sb, "b_rows", [PARTS, 3 * D])
        b_rest = both(sb, "b_rest", [PARTS, 2, 3 * D])
        b_part = both(sb, "b_part", [PARTS, PARTS, 3 * D], BF16)
        b_pick = both(sb, "b_pick", [PARTS, 2, 3 * D])
        b_bf = both(sb, "b_bf", [PARTS, 3 * D], BF16)
        lnb3 = both(sb, "lnb3", [P, PARTS])
        kbias = sb("kbias", [P, 2])
        cond_sb = sb("cond_sb", [P, E])
        cond_t = sb("cond_t", [P, E])
        cond_s = sb("cond_s", [P, E])
        condT = sb("condT", [P, EC, B])
        scale1 = both(sb, "scale1", [P, B])
        shift0 = both(sb, "shift0", [P, B])
        film_scale = both(sb, "film_scale", [P, B])
        film_shift = both(sb, "film_shift", [P, B])
        maskf_sb = sb("maskf_sb", [NT, P])
        maski_sb = sb("maski_sb", [NT, P], I32)
        masked1 = sb("masked1", [NT, P])
        kept1 = sb("kept1", [NT, P])
        neg_rest = sb("neg_rest", [NT, 3, P])
        neg_part = sb("neg_part", [NT, PARTS, P], BF16)
        neg_masked = sb("neg_masked", [NT, P], BF16)
        neg_row = [sb("neg_row0", [PARTS, B * T], BF16), sb("neg_row1", [1, B * T], BF16)]
        keep = both(sb, "keep", [P, NT])

        xs = sb("xs", [P, NT, D])
        stats = both(sb, "stats", [P, TG, 6])
        mv = both(sb, "mv", [P, TG, 2])
        mean_rstd_x = both(sb, "mean_rstd_x", [P, TG])
        var_eps = both(sb, "var_eps", [P, TG])
        rstd = both(sb, "rstd", [P, TG])
        z = both(sb, "z", [P, TG, D])
        zT = both(sb, "zT", [P, R])
        k_max = both(sb, "k_max", [P, BG])
        k_maxb = both(sb, "k_maxb", [P, BG])
        ke = both(sb, "ke", [P, BG, T])
        k_sum = both(sb, "k_sum", [P, BG])
        k_rec = both(sb, "k_rec", [P, BG])
        q_max = [sb(f"q_max{n}", [P, TG, HEADS[n]]) for n in range(2)]
        qe = both(sb, "qe", [P, TG, D])
        qT = both(sb, "qT", [P, R])
        compact = both(sb, "compact", [P, TG, D])
        spread = both(sb, "spread", [P, TG, BT, D])
        att = both(sb, "att", [P, BG, Q])
        att_bd = [sb(f"att_bd{n}", [P, BG, D + HEADS[n]]) for n in range(2)]
        q_rec = [sb(f"q_rec{n}", [P, TG, HEADS[n]]) for n in range(2)]
        y = both(sb, "y", [P, TG, D])
        stats2 = both(sb, "stats2", [P, TG, 6])
        mv2 = both(sb, "mv2", [P, TG, 2])
        var_eps2 = both(sb, "var_eps2", [P, TG])
        rstd2 = both(sb, "rstd2", [P, TG])
        mean_rstd = both(sb, "mean_rstd", [P, TG])
        yn = both(sb, "yn", [P, TG, D])
        fs = both(sb, "fs", [P, BG, T])
        fh = both(sb, "fh", [P, BG, T])
        th = both(sb, "th", [P, BG, T])
        gate = both(sb, "gate", [P, BG, T])

        ps_t = [ctx.enter_context(nc.psum_tensor(f"ps_t{n}", [P, 512], F32)) for n in range(2)]
        ps_k = [ctx.enter_context(nc.psum_tensor(f"ps_k{n}", [P, 512], F32)) for n in range(2)]
        ps_w = [ctx.enter_context(nc.psum_tensor(f"ps_w{n}", [P, 2, 512], F32)) for n in range(2)]
        wide = [w[:, :, :].rearrange("p a (b n) -> p (a b) n", b=2) for w in ps_w]

        loaded = {k: sem(f"loaded_{k}") for k in ("cond", "vectors", "w_raw", "b_rows", "w_emb", "w_out", "masks")}
        x_loaded = sem("x_loaded")
        c_ident, c_sel, c_spread, c_pool = sem("c_ident"), sem("c_sel"), sem("c_spread"), sem("c_pool")
        c_ones, c_hmask, c_attbd = sem("c_ones"), sem("c_hmask"), sem("c_attbd")
        c_win, c_wout, c_negp, c_neg, c_kept1 = sem("c_win"), sem("c_wout"), sem("c_negp"), sem("c_neg"), sem("c_kept1")
        c_negrow, c_tr, c_vcol, c_keep = sem("c_negrow"), sem("c_tr"), sem("c_vcol"), sem("c_keep")
        c_tanh, c_silu, c_cT, c_condT = sem("c_tanh"), sem("c_silu"), sem("c_cT"), sem("c_condT")
        c_film_ps, c_film1, c_film = sem("c_film_ps"), sem("c_film1"), sem("c_film")
        c_lnb3, c_bias_ps, c_bstep, c_bias, c_kb = sem("c_lnb3"), sem("c_bias_ps"), sem("c_bstep"), sem("c_bias"), sem("c_kb")

        names = ("stat", "stat_seen", "stat2_seen", "moments", "var_eps", "rstd", "mean_rstd_x", "z", "z_ps", "zT", "k_ps", "qv_ps", "k_max", "k_maxb", "k_sub",
                 "k_exp", "k_sum", "k_rec", "k_norm", "kT_ps", "q_max", "q_sub", "q_exp", "qT_ps", "qT", "compact",
                 "spread", "att_ps", "att", "att_seen", "att_bd", "y_ps", "q_rec", "y", "stat2", "moments2", "var_eps2", "rstd2",
                 "mean_rstd", "yn", "ynT_ps", "fs", "fh", "tanh", "gate", "out_ps", "done")
        S = {k: both(sem, f"s_{k}_") for k in names}
        stored = sem("stored")

        def seen(eng, name, n, g, per=1):
            eng.wait_ge(S[name][n], (g + 1) * per)

        def per_head(ap, n):
            return ap.rearrange("p t (h c) -> p t h c", h=HEADS[n])

        block = ctx.enter_context(nc.Block())

        x_v = x.rearrange("b t c -> (b t) c").rearrange("(j p) c -> p j c", p=P)
        out_v = out.rearrange("b t c -> (b t) c").rearrange("(j p) c -> p j c", p=P)

        @block.sync
        def _(sp):
            sp.dma_start(xs[:, 0:TG, :], x_v[:, 0:TG, :]).then_inc(x_loaded, 16)
            for n in range(2):
                for m, w in enumerate(("Wq", "Wv", "Wk")):
                    sp.dma_start(w_raw[n][:, m * D:(m + 1) * D], layers[n][w]).then_inc(loaded["w_raw"], 16)
            for n in range(2):
                sp.dma_start(w_out[n][:, :], layers[n]["W_out"]).then_inc(loaded["w_out"], 16)
            with sp.Fori(1, NG) as g:
                sp.wait_ge(x_loaded, g * 16)
                sp.dma_start(xs[:, bass.ds(g * TG, TG), :], x_v[:, bass.ds(g * TG, TG), :]).then_inc(x_loaded, 16)
            with sp.Fori(0, NG) as g:
                seen(sp, "done", 1, g)
                sp.dma_start(out_v[:, bass.ds(g * TG, TG), :], xs[:, bass.ds(g * TG, TG), :]).then_inc(stored, 16)
            sp.wait_ge(stored, NG * 16)

        @block.gpsimd
        def _(pool):
            g_ = nc.gpsimd
            for n in range(2):
                for row, v in ((LNW, "ln_w"), (LNB, "ln_b"), (BK, "bk"), (LN2W, "ln2_w"), (LN2B, "ln2_b")):
                    pool.dma_start(vectors[n * NVEC + row:n * NVEC + row + 1, :],
                                   layers[n][v].rearrange("(a c) -> a c", a=1)).then_inc(loaded["vectors"], 16)
                pool.dma_start(vectors[n * NVEC + BSCALE:n * NVEC + BSHIFT + 1, :],
                               layers[n]["b_emb"].rearrange("(a c) -> a c", a=2)).then_inc(loaded["vectors"], 16)
            g_.memset(ident[:, :], 0.0).then_inc(c_pool, 1)
            g_.memset(exponent[:, :], -0.5).then_inc(c_pool, 1)
            for n in range(2):
                g_.memset(head_of[n][:, :], 1.0).then_inc(c_pool, 1)
            pool.wait_ge(c_pool, 4)
            g_.affine_select(out=ident[:, :], in_=ident[:, :], compare_op=ALU.not_equal, fill=1.0, base=0,
                             pattern=[[-1, P]], channel_multiplier=1).then_inc(c_ident, 1)
            for n in range(2):
                w = D // HEADS[n]
                g_.affine_select(out=head_of[n][:, :], in_=head_of[n][:, :], compare_op=ALU.is_ge, fill=0.0, base=0,
                                 pattern=[[-w, HEADS[n]]], channel_multiplier=1).then_inc(c_sel, 1)
            for n in range(2):
                w = D // HEADS[n]
                pool.wait_ge(c_sel, n + 2)
                g_.affine_select(out=head_of[n][:, :], in_=head_of[n][:, :], compare_op=ALU.is_ge, fill=0.0,
                                 base=w - 1, pattern=[[w, HEADS[n]]], channel_multiplier=-1).then_inc(c_sel, 1)
            g_.memset(spread[0][:, :, :, :], 0.0).then_inc(c_spread, 1)
            g_.memset(att_bd[0][:, :, 0:D], 0.0).then_inc(c_attbd, 1)

            def rstd_x(n, g):
                seen(pool, "var_eps", n, g)
                g_.tensor_tensor(rstd[n][:, :], var_eps[n][:, :], exponent[:, :], ALU.pow).then_inc(S["rstd"][n], 1)
                seen(pool, "rstd", n, g)

            def scale_k(n, g):
                seen(pool, "k_rec", n, g)
                g_.tensor_tensor(ke[n][:, :, :], ke[n][:, :, :], k_rec[n][:, :].unsqueeze(2).to_broadcast([P, BG, T]),
                                 ALU.mult).then_inc(S["k_norm"][n], 1)
                seen(pool, "k_norm", n, g)

            def spread_att(n, g):
                seen(pool, "att", n, g)
                pool.sem_inc(S["att_seen"][n], 1)
                for r in range(NQ):
                    part = slice(r * Q, (r + 1) * Q)
                    g_.tensor_scalar(att_bd[n][part, :, r * Q:(r + 1) * Q], att[n][part, :, :], 1.0, 0.0,
                                     ALU.mult, ALU.add).then_inc(S["att_bd"][n], 1)
                seen(pool, "att_bd", n, g, NQ)

            def rstd_y(n, g):
                seen(pool, "var_eps2", n, g)
                g_.tensor_tensor(rstd2[n][:, :], var_eps2[n][:, :], exponent[:, :], ALU.pow).then_inc(S["rstd2"][n], 1)
                seen(pool, "rstd2", n, g)

            def film_add(n, g):
                seen(pool, "fs", n, g)
                g_.tensor_tensor(fh[n][:, :, :], fs[n][:, :, :],
                                 film_shift[n][:, bass.ds(g * BG, BG)].unsqueeze(2).to_broadcast([P, BG, T]),
                                 ALU.add).then_inc(S["fh"][n], 1)
                seen(pool, "fh", n, g)

            steps = (rstd_x, scale_k, spread_att, rstd_y, film_add)
            for step in steps:
                if step is spread_att:
                    pool.wait_ge(c_attbd, 1)
                if step is film_add:
                    pool.wait_ge(c_film, 2)
                step(0, 0)
            g_.memset(spread[1][:, :, :, :], 0.0).then_inc(c_spread, 1)
            g_.memset(att_bd[1][:, :, 0:D], 0.0).then_inc(c_attbd, 1)
            pool.wait_ge(c_attbd, 2)
            with pool.Fori(1, NG) as g:
                for step in steps:
                    step(0, g)
                    step(1, g - 1)
            for step in steps:
                step(1, NG - 1)

        @block.scalar
        def _(act):
            a_ = nc.scalar
            act.dma_start(cond_sb[:, :], cond).then_inc(loaded["cond"], 16)
            act.dma_start(maskf_sb[:, :], mask_f.rearrange("b t a -> (b t a)").rearrange("(j p) -> j p", p=P)).then_inc(loaded["masks"], 16)
            act.dma_start(maski_sb[:, :], mask_i.rearrange("b t -> (b t)").rearrange("(j p) -> j p", p=P)).then_inc(loaded["masks"], 16)
            for n in range(2):
                for m, v in enumerate(("bq", "bv", "b_out")):
                    for i in range(PARTS):
                        act.dma_start(b_rows[n][i:i + 1, m * D:(m + 1) * D],
                                      layers[n][v].rearrange("(a c) -> a c", a=1)).then_inc(loaded["b_rows"], 16)
            for n in range(2):
                act.dma_start(w_emb[n][:, :, :], layers[n]["W_emb"].rearrange("(k p) m -> p k m", p=P)).then_inc(loaded["w_emb"], 16)
            act.wait_ge(loaded["cond"], 16)
            a_.activation(cond_t[:, :], cond_sb[:, :], ACT.Tanh, scale=0.5).then_inc(c_tanh, 1)
            act.wait_ge(c_neg, 4)
            for i in range(PARTS):
                act.dma_start(neg_row[0][i:i + 1, :].rearrange("a (j p) -> a j p", p=P),
                              neg_part[:, i:i + 1, :].rearrange("j a p -> j (a p)")).then_inc(c_negrow, 16)
            act.dma_start(neg_row[1][0:1, :].rearrange("a (j p) -> a j p", p=P), neg_masked[:, :]).then_inc(c_negrow, 16)

            def normalise_x(n, g):
                seen(act, "mean_rstd_x", n, g)
                seen(act, "rstd", n, g)
                if n == 0:
                    act.wait_ge(x_loaded, (g + 1) * 16)
                else:
                    seen(act, "done", 0, g)
                for j in range(TG):
                    a_.activation(z[n][:, j, :], xs[:, bass.ds(g * TG + j, 1), :].rearrange("p a c -> p (a c)"),
                                  ACT.Identity, scale=rstd[n][:, j:j + 1], bias=mean_rstd_x[n][:, j:j + 1]
                                  ).then_inc(S["z"][n], 1)

            def copy_zT(n, g):
                seen(act, "z_ps", n, g)
                a_.copy(zT[n][:, :], ps_t[n][:, :]).then_inc(S["zT"][n], 1)

            def exp_k(n, g):
                seen(act, "k_sub", n, g)
                a_.activation(ke[n][:, :, :], ke[n][:, :, :], ACT.Exp).then_inc(S["k_exp"][n], 1)

            def exp_q(n, g):
                seen(act, "q_sub", n, g)
                a_.activation(qe[n][:, :, :], qe[n][:, :, :], ACT.Exp).then_inc(S["q_exp"][n], 1)

            def copy_v(n, g):
                seen(act, "qv_ps", n, g)
                v = ps_w[n][:, 1, :].rearrange("p (j c) -> p j c", j=TG)
                if n == 0:
                    for r in range(NQ):
                        part = slice(r * Q, (r + 1) * Q)
                        a_.copy(spread[0][part, :, r, :], v[part, :, :]).then_inc(S["spread"][0], 1)
                else:
                    for j in range(TG):
                        a_.activation(compact[1][:, j, :], v[:, j, :], ACT.Copy,
                                      scale=keep[1][:, bass.ds(g * TG + j, 1)]).then_inc(S["compact"][1], 1)

            def copy_k(n, g):
                seen(act, "kT_ps", n, g)
                k = ps_k[n][:, :].rearrange("p (j c) -> p j c", j=TG)
                if n == 0:
                    for j in range(TG):
                        a_.activation(compact[0][:, j, :], k[:, j, :], ACT.Copy,
                                      scale=keep[0][:, bass.ds(g * TG + j, 1)]).then_inc(S["compact"][0], 1)
                else:
                    for r in range(NQ):
                        part = slice(r * Q, (r + 1) * Q)
                        a_.copy(spread[1][part, :, r, :], k[part, :, :]).then_inc(S["spread"][1], 1)

            def copy_qT(n, g):
                seen(act, "qT_ps", n, g)
                a_.copy(qT[n][:, :], ps_t[n][:, :]).then_inc(S["qT"][n], 1)

            def normalise_y(n, g):
                seen(act, "mean_rstd", n, g)
                seen(act, "rstd2", n, g)
                seen(act, "y", n, g)
                for j in range(TG):
                    a_.activation(yn[n][:, j, :], y[n][:, j, :], ACT.Identity, scale=rstd2[n][:, j:j + 1],
                                  bias=mean_rstd[n][:, j:j + 1]).then_inc(S["yn"][n], 1)

            def tanh_h(n, g):
                seen(act, "fh", n, g)
                a_.activation(th[n][:, :, :], fh[n][:, :, :], ACT.Tanh, scale=0.5).then_inc(S["tanh"][n], 1)

            steps = (normalise_x, copy_zT, copy_v, exp_k, exp_q, copy_qT, copy_k, normalise_y, tanh_h)
            for step in steps:
                if step is copy_v:
                    act.wait_ge(c_spread, 1)
                if step is copy_k:
                    act.wait_ge(c_keep, 2)
                step(0, 0)
            act.wait_ge(c_spread, 2)
            with act.Fori(1, NG) as g:
                for step in steps:
                    step(0, g)
                    step(1, g - 1)
            for step in steps:
                step(1, NG - 1)

        @block.vector
        def _(dve):
            v_ = nc.vector
            v_.memset(ones3[:, :], 1.0).then_inc(c_ones, 1)

            def x_stats(n, g):
                if n == 0:
                    dve.wait_ge(x_loaded, (g + 1) * 16)
                else:
                    seen(dve, "done", 0, g)
                for j in range(TG):
                    v_.bn_stats(stats[n][:, j, :], xs[:, bass.ds(g * TG + j, 1), :].rearrange("p a c -> p (a c)")
                                ).then_inc(S["stat"][n], 1)
                seen(dve, "stat", n, g, TG)
                dve.sem_inc(S["stat_seen"][n], 1)
                for j in range(TG):
                    v_.bn_aggr(mv[n][:, j, :], stats[n][:, j, :]).then_inc(S["moments"][n], 1)
                seen(dve, "moments", n, g, TG)
                v_.tensor_scalar(var_eps[n][:, :], mv[n][:, :, 1], EPS, None, ALU.add).then_inc(S["var_eps"][n], 1)
                seen(dve, "rstd", n, g)
                v_.scalar_tensor_tensor(mean_rstd_x[n][:, :], mv[n][:, :, 0], -1.0, rstd[n][:, :], ALU.mult, ALU.mult
                                        ).then_inc(S["mean_rstd_x"][n], 1)

            def k_softmax_in(n, g):
                seen(dve, "k_ps", n, g)
                k = ps_k[n][:, :].rearrange("p (b t) -> p b t", t=T)
                v_.tensor_reduce(k_max[n][:, :], k, X, ALU.max).then_inc(S["k_max"][n], 1)
                seen(dve, "k_max", n, g)
                v_.tensor_scalar(k_maxb[n][:, :], k_max[n][:, :], kbias[:, n:n + 1], None, ALU.add
                                 ).then_inc(S["k_maxb"][n], 1)
                seen(dve, "k_maxb", n, g)
                v_.scalar_tensor_tensor(ke[n][:, :, :], k, kbias[:, n:n + 1],
                                        k_maxb[n][:, :].unsqueeze(2).to_broadcast([P, BG, T]),
                                        ALU.add, ALU.subtract).then_inc(S["k_sub"][n], 1)

            def q_softmax_in(n, g):
                seen(dve, "qv_ps", n, g)
                q = per_head(ps_w[n][:, 0, :].rearrange("p (j c) -> p j c", j=TG), n)
                v_.tensor_reduce(q_max[n][:, :, :], q, X, ALU.max).then_inc(S["q_max"][n], 1)
                seen(dve, "q_max", n, g)
                v_.tensor_tensor(per_head(qe[n][:, :, :], n), q,
                                 q_max[n][:, :, :].unsqueeze(3).to_broadcast([P, TG, HEADS[n], D // HEADS[n]]),
                                 ALU.subtract).then_inc(S["q_sub"][n], 1)

            def k_sums(n, g):
                seen(dve, "k_exp", n, g)
                v_.tensor_reduce(k_sum[n][:, :], ke[n][:, :, :], X, ALU.add).then_inc(S["k_sum"][n], 1)
                seen(dve, "k_sum", n, g)
                v_.reciprocal(k_rec[n][:, :], k_sum[n][:, :]).then_inc(S["k_rec"][n], 1)

            def mask_att(n, g):
                seen(dve, "att_ps", n, g)
                v_.tensor_tensor(att[n][:, :, :], ps_k[n][:, :].rearrange("p (b c) -> p b c", c=Q),
                                 head_mask[n][:, :].unsqueeze(1).to_broadcast([P, BG, Q]), ALU.mult
                                 ).then_inc(S["att"][n], 1)

            def y_stats(n, g):
                seen(dve, "y_ps", n, g)
                v_.reciprocal(q_rec[n][:, :, :], wide[n][:, :, D:D + HEADS[n]]).then_inc(S["q_rec"][n], 1)
                seen(dve, "q_rec", n, g)
                v_.tensor_tensor(per_head(y[n][:, :, :], n), per_head(wide[n][:, :, 0:D], n),
                                 q_rec[n][:, :, :].unsqueeze(3).to_broadcast([P, TG, HEADS[n], D // HEADS[n]]),
                                 ALU.mult).then_inc(S["y"][n], 1)
                seen(dve, "y", n, g)
                for j in range(TG):
                    v_.bn_stats(stats2[n][:, j, :], y[n][:, j, :]).then_inc(S["stat2"][n], 1)
                seen(dve, "stat2", n, g, TG)
                dve.sem_inc(S["stat2_seen"][n], 1)
                for j in range(TG):
                    v_.bn_aggr(mv2[n][:, j, :], stats2[n][:, j, :]).then_inc(S["moments2"][n], 1)
                seen(dve, "moments2", n, g, TG)
                v_.tensor_scalar(var_eps2[n][:, :], mv2[n][:, :, 1], EPS, None, ALU.add).then_inc(S["var_eps2"][n], 1)
                seen(dve, "rstd2", n, g)
                v_.scalar_tensor_tensor(mean_rstd[n][:, :], mv2[n][:, :, 0], -1.0, rstd2[n][:, :], ALU.mult, ALU.mult
                                        ).then_inc(S["mean_rstd"][n], 1)

            def film_mul(n, g):
                seen(dve, "ynT_ps", n, g)
                v_.tensor_tensor(fs[n][:, :, :], ps_t[n][:, :].rearrange("p (b t) -> p b t", t=T),
                                 film_scale[n][:, bass.ds(g * BG, BG)].unsqueeze(2).to_broadcast([P, BG, T]),
                                 ALU.mult).then_inc(S["fs"][n], 1)

            def gate_h(n, g):
                seen(dve, "tanh", n, g)
                seen(dve, "fh", n, g)
                v_.scalar_tensor_tensor(gate[n][:, :, :], th[n][:, :, :], 1.0, fh[n][:, :, :], ALU.add, ALU.mult
                                        ).then_inc(S["gate"][n], 1)

            def residual(n, g):
                seen(dve, "out_ps", n, g)
                rows = xs[:, bass.ds(g * TG, TG), :]
                v_.tensor_tensor(rows, ps_k[n][:, :].rearrange("p (j c) -> p j c", j=TG), rows, ALU.add
                                 ).then_inc(S["done"][n], 1)

            def setup_weights():
                dve.wait_ge(c_vcol, 1)
                dve.wait_ge(loaded["w_raw"], 6 * 16)
                dve.wait_ge(loaded["w_out"], 2 * 16)
                for n in range(2):
                    v_.tensor_copy(lnb3[n][:, :], vcol[:, n * NVEC + LNB:n * NVEC + LNB + 1].to_broadcast([P, PARTS])
                                   ).then_inc(c_lnb3, 1)
                for n in range(2):
                    v_.tensor_scalar(w_in[n][:, :], w_raw[n][:, :], vcol[:, n * NVEC + LNW:n * NVEC + LNW + 1], None,
                                     ALU.mult).then_inc(c_win, 1)
                    v_.tensor_scalar(w_out[n][:, :], w_out[n][:, :], 0.5, None, ALU.mult).then_inc(c_wout, 1)

            def setup_masks():
                dve.wait_ge(loaded["masks"], 2 * 16)
                v_.tensor_scalar(neg_rest[:, 0, :], maskf_sb[:, :], -1.0, 1000000.0, ALU.add, ALU.mult).then_inc(c_negp, 1)
                v_.tensor_scalar(masked1[:, :], maski_sb[:, :], 1.0, None, ALU.is_equal).then_inc(c_negp, 1)
                dve.wait_ge(c_negp, 2)
                v_.tensor_scalar(kept1[:, :], masked1[:, :], -1.0, 1.0, ALU.mult, ALU.add).then_inc(c_kept1, 1)
                v_.tensor_scalar(neg_masked[:, :], masked1[:, :], -1e30, None, ALU.mult).then_inc(c_neg, 1)
                v_.tensor_copy(neg_part[:, 0, :], neg_rest[:, 0, :]).then_inc(c_neg, 1)
                for i in (1, 2):
                    dve.wait_ge(c_neg, i + 1)
                    v_.tensor_tensor(neg_rest[:, i, :], neg_rest[:, i - 1, :], neg_part[:, i - 1, :], ALU.subtract
                                     ).then_inc(c_negp, 1)
                    dve.wait_ge(c_negp, 2 + i)
                    v_.tensor_copy(neg_part[:, i, :], neg_rest[:, i, :]).then_inc(c_neg, 1)

            def setup_columns():
                dve.wait_ge(c_tr, 1)
                v_.tensor_copy(vcol[:, :], ps_t[1][:, 0:2 * NVEC]).then_inc(c_vcol, 1)
                for n in range(2):
                    v_.tensor_copy(keep[n][:, :], ps_t[1][:, 32 + n * NT:32 + (n + 1) * NT]).then_inc(c_keep, 1)
                dve.wait_ge(c_sel, 4)
                for n in range(2):
                    w = D // HEADS[n]
                    for r in range(NQ):
                        part = slice(r * Q, (r + 1) * Q)
                        hs = head_of[n][part, r * Q // w:(r + 1) * Q // w]
                        v_.tensor_copy(head_mask[n][part, :].rearrange("p (h c) -> p h c", c=w),
                                       hs.unsqueeze(2).to_broadcast([Q, Q // w, w])).then_inc(c_hmask, 1)
                    v_.tensor_copy(att_bd[n][:, :, D:D + HEADS[n]],
                                   head_of[n][:, :].unsqueeze(1).to_broadcast([P, BG, HEADS[n]])).then_inc(c_hmask, 1)

            def setup_biases():
                dve.wait_ge(c_bias_ps, 1)
                dve.wait_ge(loaded["b_rows"], 2 * 9 * 16)
                for n in range(2):
                    v_.tensor_tensor(b_rest[n][:, 0, 0:2 * D], ps_w[1][0:PARTS, 0, n * 2 * D:(n + 1) * 2 * D],
                                     b_rows[n][:, 0:2 * D], ALU.add).then_inc(c_bstep, 1)
                    v_.tensor_copy(b_rest[n][:, 0, 2 * D:3 * D], b_rows[n][:, 2 * D:3 * D]).then_inc(c_bstep, 1)
                    v_.tensor_scalar(kbias[:, n:n + 1], ps_w[1][:, 1, n:n + 1], vcol[:, n * NVEC + BK:n * NVEC + BK + 1],
                                     None, ALU.add).then_inc(c_kb, 1)
                dve.wait_ge(c_bstep, 4)
                count = 4
                for n in range(2):
                    v_.tensor_copy(b_part[n][:, 0, :], b_rest[n][:, 0, :]).then_inc(c_bstep, 1)
                    count += 1
                    for src, dst, i in ((0, 1, 1), (1, 0, 2)):
                        dve.wait_ge(c_bstep, count)
                        v_.tensor_tensor(b_rest[n][:, dst, :], b_rest[n][:, src, :], b_part[n][:, i - 1, :], ALU.subtract
                                         ).then_inc(c_bstep, 1)
                        dve.wait_ge(c_bstep, count + 1)
                        v_.tensor_copy(b_part[n][:, i, :], b_rest[n][:, dst, :]).then_inc(c_bstep, 1)
                        count += 2
                    dve.wait_ge(c_bstep, count)
                    v_.tensor_scalar(b_pick[n][:, 0, :], b_part[n][:, 0, :], ident[0:PARTS, 0:1], None, ALU.mult
                                     ).then_inc(c_bstep, 1)
                    dve.wait_ge(c_bstep, count + 1)
                    v_.scalar_tensor_tensor(b_pick[n][:, 1, :], b_part[n][:, 1, :], ident[0:PARTS, 1:2],
                                            b_pick[n][:, 0, :], ALU.mult, ALU.add).then_inc(c_bstep, 1)
                    dve.wait_ge(c_bstep, count + 2)
                    v_.scalar_tensor_tensor(b_bf[n][:, :], b_part[n][:, 2, :], ident[0:PARTS, 2:3],
                                            b_pick[n][:, 1, :], ALU.mult, ALU.add).then_inc(c_bias, 1)
                    count += 2

            def setup_silu():
                dve.wait_ge(c_tanh, 1)
                v_.scalar_tensor_tensor(cond_s[:, :], cond_t[:, :], 1.0, cond_sb[:, :], ALU.add, ALU.mult
                                        ).then_inc(c_silu, 1)
                dve.wait_ge(c_cT, 1)
                v_.tensor_scalar(condT[:, :, :], ps_t[1][:, 128:128 + EC * B].rearrange("p (k b) -> p k b", k=EC), 0.5,
                                 None, ALU.mult).then_inc(c_condT, 1)

            def setup_film():
                dve.wait_ge(c_film_ps, 1)
                for n in range(2):
                    col = n * NVEC
                    v_.tensor_scalar(scale1[n][:, :], ps_k[1][:, 2 * n * B:(2 * n + 1) * B],
                                     vcol[:, col + BSCALE:col + BSCALE + 1], 1.0, ALU.add, ALU.add).then_inc(c_film1, 1)
                    v_.tensor_scalar(shift0[n][:, :], ps_k[1][:, (2 * n + 1) * B:(2 * n + 2) * B],
                                     vcol[:, col + BSHIFT:col + BSHIFT + 1], None, ALU.add).then_inc(c_film1, 1)
                dve.wait_ge(c_film1, 4)
                for n in range(2):
                    col = n * NVEC
                    v_.tensor_scalar(film_scale[n][:, :], scale1[n][:, :], vcol[:, col + LN2W:col + LN2W + 1], None,
                                     ALU.mult).then_inc(c_film, 1)
                    v_.scalar_tensor_tensor(film_shift[n][:, :], scale1[n][:, :], vcol[:, col + LN2B:col + LN2B + 1],
                                            shift0[n][:, :], ALU.mult, ALU.add).then_inc(c_film, 1)

            x_stats(0, 0)
            setup_masks()
            setup_columns()
            setup_weights()
            setup_biases()
            dve.wait_ge(c_kb, 2)
            k_softmax_in(0, 0)
            q_softmax_in(0, 0)
            k_sums(0, 0)
            setup_silu()
            dve.wait_ge(c_hmask, 2 * NQ + 2)
            mask_att(0, 0)
            setup_film()
            y_stats(0, 0)
            dve.wait_ge(c_film, 4)
            film_mul(0, 0)
            gate_h(0, 0)
            residual(0, 0)
            steps = (x_stats, k_softmax_in, q_softmax_in, k_sums, mask_att, y_stats, film_mul, gate_h, residual)
            with dve.Fori(1, NG) as g:
                for step in steps:
                    step(0, g)
                    step(1, g - 1)
            for step in steps:
                step(1, NG - 1)

        @block.tensor
        def _(pe):
            t_ = nc.tensor

            def transpose_rows(src, dst):
                for j in range(TG):
                    last = t_.transpose(dst[:, j * P:(j + 1) * P], src[:, j, :], ident[:, :])
                return last

            def z_transpose(n, g):
                seen(pe, "z", n, g, TG)
                transpose_rows(z[n], ps_t[n]).then_inc(S["z_ps"][n], 1)

            def project(n, g):
                seen(pe, "zT", n, g)
                t_.matmul(ps_k[n][:, :], w_in[n][:, 2 * D:3 * D], zT[n][:, :], start=True, stop=False)
                parts = PARTS if n == 0 else 1
                t_.matmul(ps_k[n][:, :], ones3[0:parts, :], neg_row[n][0:parts, bass.ds(g * R, R)], start=False,
                          stop=True).then_inc(S["k_ps"][n], 1)
                for m in range(2):
                    t_.matmul(ps_w[n][:, m, :], ones3[:, :],
                              b_bf[n][:, m * D:(m + 1) * D].unsqueeze(1).to_broadcast([PARTS, TG, D]),
                              start=True, stop=False)
                    for j in range(TG):
                        last = t_.matmul(ps_w[n][:, m, j * D:(j + 1) * D], zT[n][:, j * P:(j + 1) * P],
                                         w_in[n][:, m * D:(m + 1) * D], start=False, stop=j == TG - 1)
                last.then_inc(S["qv_ps"][n], 1)

            def k_transpose(n, g):
                seen(pe, "k_norm", n, g)
                transpose_rows(ke[n][:, :, :].rearrange("p (j b) t -> p j (b t)", j=TG), ps_k[n]
                               ).then_inc(S["kT_ps"][n], 1)

            def q_transpose(n, g):
                seen(pe, "q_exp", n, g)
                transpose_rows(qe[n], ps_t[n]).then_inc(S["qT_ps"][n], 1)

            def attend(n, g):
                seen(pe, "compact", n, g, TG)
                seen(pe, "spread", n, g, NQ)
                for j in range(TG):
                    for r in range(NQ):
                        last = t_.matmul(ps_k[n][r * Q:(r + 1) * Q, j * P:(j + 1) * P],
                                         compact[n][:, j, r * Q:(r + 1) * Q], spread[n][:, j, :, r * Q:(r + 1) * Q],
                                         start=True, stop=True, tile_position=(0, r * Q))
                last.then_inc(S["att_ps"][n], 1)

            def read_out(n, g):
                seen(pe, "att_bd", n, g, NQ)
                seen(pe, "qT", n, g)
                for b in range(BG):
                    j, r = b // BT, b % BT
                    last = t_.matmul(wide[n][r * T:(r + 1) * T, j, 0:D + HEADS[n]], qT[n][:, b * T:(b + 1) * T],
                                     att_bd[n][:, b, :], start=True, stop=True, tile_position=(0, r * T))
                last.then_inc(S["y_ps"][n], 1)

            def y_transpose(n, g):
                seen(pe, "yn", n, g, TG)
                transpose_rows(yn[n], ps_t[n]).then_inc(S["ynT_ps"][n], 1)

            def project_out(n, g):
                seen(pe, "gate", n, g)
                h = gate[n][:, :, :].rearrange("p (j b) t -> p j (b t)", j=TG)
                t_.matmul(ps_k[n][:, :], ones3[:, :],
                          b_bf[n][:, 2 * D:3 * D].unsqueeze(1).to_broadcast([PARTS, TG, D]), start=True, stop=False)
                for j in range(TG):
                    last = t_.matmul(ps_k[n][:, j * P:(j + 1) * P], h[:, j, :], w_out[n][:, :], start=False,
                                     stop=j == TG - 1)
                last.then_inc(S["out_ps"][n], 1)

            pe.wait_ge(c_ident, 1)
            pe.wait_ge(loaded["vectors"], 12 * 16)
            pe.wait_ge(loaded["masks"], 2 * 16)
            pe.wait_ge(c_kept1, 1)
            t_.transpose(ps_t[1][:, 0:2 * NVEC], vectors[:, :], ident[0:2 * NVEC, 0:2 * NVEC])
            t_.transpose(ps_t[1][:, 32:32 + NT], maskf_sb[:, :], ident[0:NT, 0:NT])
            t_.transpose(ps_t[1][:, 32 + NT:32 + 2 * NT], kept1[:, :], ident[0:NT, 0:NT]).then_inc(c_tr, 1)
            pe.wait_ge(c_lnb3, 2)
            for n in range(2):
                t_.matmul(ps_w[1][0:PARTS, 0, n * 2 * D:(n + 1) * 2 * D], lnb3[n][:, :], w_raw[n][:, 0:2 * D],
                          start=True, stop=True)
            for n in range(2):
                last = t_.matmul(ps_w[1][:, 1, n:n + 1], w_raw[n][:, 2 * D:3 * D], lnb3[n][:, 0:1], start=True, stop=True)
            last.then_inc(c_bias_ps, 1)
            z_transpose(0, 0)
            pe.wait_ge(c_ones, 1)
            pe.wait_ge(c_win, 2)
            pe.wait_ge(c_bias, 2)
            pe.wait_ge(c_negrow, 4 * 16)
            project(0, 0)
            pe.wait_ge(c_silu, 1)
            for k in range(EC):
                last = t_.transpose(ps_t[1][:, 128 + k * B:128 + (k + 1) * B], cond_s[:, k * P:(k + 1) * P], ident[:, :])
            last.then_inc(c_cT, 1)
            q_transpose(0, 0)
            k_transpose(0, 0)
            pe.wait_ge(c_condT, 1)
            pe.wait_ge(loaded["w_emb"], 2 * 16)
            for n in range(2):
                for half in range(2):
                    for k in range(EC):
                        last = t_.matmul(ps_k[1][:, (2 * n + half) * B:(2 * n + half + 1) * B],
                                         w_emb[n][:, k, half * D:(half + 1) * D], condT[:, k, :],
                                         start=(k == 0), stop=(k == EC - 1))
            last.then_inc(c_film_ps, 1)
            attend(0, 0)
            pe.wait_ge(c_hmask, 2 * NQ + 2)
            read_out(0, 0)
            y_transpose(0, 0)
            pe.wait_ge(c_wout, 2)
            project_out(0, 0)
            steps = (z_transpose, project, q_transpose, k_transpose, attend, read_out, y_transpose, project_out)
            with pe.Fori(1, NG) as g:
                for step in steps:
                    step(0, g)
                    step(1, g - 1)
            for step in steps:
                step(1, NG - 1)


_L0 = {"ln_w": "L0_cond_ln_w", "ln_b": "L0_cond_ln_b", "Wq": "L0_cond_Wq", "bq": "L0_cond_bq", "Wk": "L0_cond_Wk",
       "bk": "L0_cond_bk", "Wv": "L0_cond_Wv", "bv": "L0_cond_bv", "W_emb": "L0_cond_W_emb", "b_emb": "L0_cond_b_emb",
       "ln2_w": "L0_cond_ln2_w", "ln2_b": "L0_cond_ln2_b", "W_out": "L0_cond_W_out", "b_out": "L0_cond_b_out"}
_L1 = {"ln_w": "L1_cond_norm_scale", "ln_b": "L1_cond_norm_bias", "Wq": "L1_cond_Wq", "bq": "L1_cond_bq",
       "Wk": "L1_cond_Wk", "bk": "L1_cond_bk", "Wv": "L1_cond_Wv", "bv": "L1_cond_bv", "W_emb": "L1_cond_film_emb_W",
       "b_emb": "L1_cond_film_emb_b", "ln2_w": "L1_cond_film_norm_scale", "ln2_b": "L1_cond_film_norm_bias",
       "W_out": "L1_cond_film_out_W", "b_out": "L1_cond_film_out_b"}


def kernel(**inputs):
    import numpy as np
    import concourse.bacc as bacc
    from concourse.bass_utils import run_bass_kernel_spmd

    nc = bacc.Bacc("TRN2", target_bir_lowering=False, num_devices=1)
    arrays, aps = {}, {}
    for name in ["x", "cond_2048", "mask_BxSx1_fk1", "mask_BxS_ik0", *_L0.values(), *_L1.values()]:
        a = np.ascontiguousarray(inputs[name])
        arrays[f"in_{name}"] = a
        aps[name] = nc.dram_tensor(f"in_{name}", a.shape, mybir.dt.from_np(a.dtype), kind="ExternalInput").ap()
    out = nc.dram_tensor("out_0", (B, T, D), F32, kind="ExternalOutput").ap()
    layers = [{k: aps[v] for k, v in names.items()} for names in (_L0, _L1)]
    build(nc, aps["x"], aps["cond_2048"], aps["mask_BxSx1_fk1"], aps["mask_BxS_ik0"], layers, out)
    r = run_bass_kernel_spmd(nc, [arrays], core_ids=[0])
    return r.results[0]["out_0"]
```

```python
from contextlib import ExitStack

import concourse.bass as bass
from concourse import mybir

F32 = mybir.dt.float32
BF16 = mybir.dt.bfloat16
I32 = mybir.dt.int32
ALU = mybir.AluOpType
ACT = mybir.ActivationFunctionType
X = mybir.AxisListType.X

P = 128
B, T, D = 128, 32, 128
E = 256
EC = E // P
NT = B * T // P
TG = 4
NG = NT // TG
BT = P // T
BG = BT * TG
R = TG * P
Q = 32
NQ = P // Q
HEADS = (8, 16)
EPS = 1e-5
PARTS = 3

LNW, LNB, BK, BSCALE, BSHIFT, LN2W, LN2B = range(7)
NVEC = 7


ORDER = {
    "tensor": (
        ("z_transpose", 1, 2),
        ("project_k", 1, 2),
        ("project_q", 1, 2),
        ("project_v", 1, 2),
        ("z_transpose", 0, 0),
        ("project_out", 1, 4),
        ("project_k", 0, 0),
        ("project_q", 0, 0),
        ("project_v", 0, 0),
        ("y_transpose", 0, 1),
        ("q_transpose", 1, 2),
        ("read_out", 1, 3),
        ("q_transpose", 0, 0),
        ("k_transpose", 0, 0),
        ("k_transpose", 1, 2),
        ("attend", 0, 0),
        ("project_out", 0, 1),
        ("attend", 1, 2),
        ("y_transpose", 1, 3),
        ("read_out", 0, 0),
    ),
    "scalar": (
        ("tanh_h", 1, 4),
        ("copy_zT", 1, 2),
        ("normalise_x", 0, 0),
        ("copy_v", 1, 2),
        ("copy_zT", 0, 0),
        ("normalise_y", 0, 1),
        ("exp_k", 1, 2),
        ("exp_q", 1, 2),
        ("exp_k", 0, 0),
        ("exp_q", 0, 0),
        ("copy_v", 0, 0),
        ("copy_qT", 0, 0),
        ("copy_k", 0, 0),
        ("tanh_h", 0, 1),
        ("copy_qT", 1, 2),
        ("copy_k", 1, 2),
        ("normalise_y", 1, 3),
        ("normalise_x", 1, 1),
    ),
    "vector": (
        ("x_stats", 0, 0),
        ("y_div", 0, 1),
        ("y_stats", 0, 1),
        ("mean_rstd_x", 0, 0),
        ("k_in", 1, 2),
        ("gate_h", 1, 4),
        ("mean_rstd", 0, 1),
        ("q_in", 1, 2),
        ("residual", 1, 4),
        ("k_in", 0, 0),
        ("q_in", 0, 0),
        ("k_sums", 0, 0),
        ("film_mul", 0, 1),
        ("k_sums", 1, 2),
        ("y_div", 1, 3),
        ("y_stats", 1, 3),
        ("gate_h", 0, 1),
        ("mean_rstd", 1, 3),
        ("mask_att", 0, 0),
        ("residual", 0, 1),
        ("x_stats", 1, 1),
        ("mask_att", 1, 2),
        ("film_mul", 1, 3),
        ("mean_rstd_x", 1, 1),
    ),
    "pool": (
        ("rstd_x", 0, 0),
        ("spread_att", 1, 3),
        ("rstd_y", 0, 1),
        ("scale_k", 0, 0),
        ("film_add", 0, 1),
        ("scale_k", 1, 2),
        ("rstd_y", 1, 3),
        ("spread_att", 0, 0),
        ("rstd_x", 1, 1),
        ("film_add", 1, 3),
    ),
}
LAGS = [entry for order in ORDER.values() for entry in order]
PRODUCTS = {
    ("z_transpose", 0): (0, (("y", 0, -1, 1), ("att", 0, -1, 1), ("qT", 0, -1, 1), ("fs", 0, -2, 1), ("k_sub", 0, -1, 1), ("zT", 0, -1, 1),)),
    ("project_k", 0): (0, (("zT", 0, 0, 1), ("y", 0, -1, 1), ("att", 0, -1, 1), ("qT", 0, -1, 1), ("fs", 0, -2, 1), ("k_sub", 0, -1, 1),)),
    ("project_q", 0): (1, (("k_sub", 1, -2, 1), ("y", 0, -1, 1), ("done", 0, -2, 1), ("compact", 0, -1, 4), ("q_sub", 0, -1, 1),)),
    ("project_v", 0): (2, (("q_sub", 1, -2, 1), ("zT", 1, -2, 1), ("att", 1, -3, 1), ("spread", 1, -3, 4), ("spread", 0, -1, 4),)),
    ("q_transpose", 0): (0, (("fs", 0, -1, 1), ("k_sub", 0, 0, 1), ("zT", 0, 0, 1), ("y", 0, -1, 1), ("att", 0, -1, 1), ("qT", 0, -1, 1),)),
    ("k_transpose", 0): (1, (("q_sub", 0, 0, 1), ("k_sub", 1, -2, 1), ("y", 0, -1, 1), ("done", 0, -2, 1), ("compact", 0, -1, 4),)),
    ("attend", 0): (0, (("qT", 0, 0, 1), ("fs", 0, -1, 1), ("k_sub", 0, 0, 1), ("zT", 0, 0, 1), ("y", 0, -1, 1), ("att", 0, -1, 1),)),
    ("read_out", 0): (0, (("done", 0, -1, 1), ("att", 0, 0, 1), ("compact", 0, 0, 4), ("qT", 0, 0, 1), ("fs", 0, -1, 1), ("q_sub", 0, 0, 1), ("k_sub", 0, 0, 1), ("zT", 0, 0, 1), ("k_sub", 1, -2, 1), ("y", 0, -1, 1),)),
    ("y_transpose", 0): (0, (("k_sub", 0, 1, 1), ("zT", 0, 1, 1), ("y", 0, 0, 1), ("att", 0, 0, 1), ("qT", 0, 0, 1), ("fs", 0, -1, 1),)),
    ("project_out", 0): (1, (("compact", 0, 1, 4), ("q_sub", 0, 1, 1), ("k_sub", 1, -1, 1), ("y", 0, 0, 1), ("done", 0, -1, 1),)),
    ("z_transpose", 1): (2, (("att", 1, -1, 1), ("spread", 1, -1, 4), ("spread", 0, 1, 4), ("q_sub", 1, -1, 1), ("zT", 1, -1, 1),)),
    ("project_k", 1): (1, (("y", 0, 1, 1), ("done", 0, 0, 1), ("compact", 0, 1, 4), ("q_sub", 0, 1, 1), ("k_sub", 1, -1, 1),)),
    ("project_q", 1): (2, (("zT", 1, 0, 1), ("att", 1, -1, 1), ("spread", 1, -1, 4), ("spread", 0, 1, 4), ("q_sub", 1, -1, 1),)),
    ("project_v", 1): (3, (("fs", 1, -2, 1), ("qT", 1, -1, 1), ("compact", 1, -1, 4),)),
    ("q_transpose", 1): (3, (("compact", 1, 0, 4), ("fs", 1, -2, 1), ("qT", 1, -1, 1),)),
    ("k_transpose", 1): (2, (("spread", 0, 2, 4), ("q_sub", 1, 0, 1), ("zT", 1, 0, 1), ("att", 1, -1, 1), ("spread", 1, -1, 4),)),
    ("attend", 1): (2, (("spread", 1, 0, 4), ("spread", 0, 2, 4), ("q_sub", 1, 0, 1), ("zT", 1, 0, 1), ("att", 1, -1, 1),)),
    ("read_out", 1): (4, (("done", 1, -1, 1), ("y", 1, -1, 1),)),
    ("y_transpose", 1): (3, (("qT", 1, 1, 1), ("compact", 1, 1, 4), ("fs", 1, -1, 1),)),
    ("project_out", 1): (4, (("y", 1, 0, 1), ("done", 1, -1, 1),)),
}


def build(nc, x, cond, mask_f, mask_i, layers, out):
    ctx = ExitStack()
    with ctx:
        def sb(name, shape, dt=F32):
            return ctx.enter_context(nc.sbuf_tensor(name, shape, dt))

        def both(make, name, *args):
            return [make(f"{name}{n}", *args) for n in range(2)]

        def sem(name):
            return ctx.enter_context(nc.semaphore(name))

        ident = sb("ident", [P, P])
        head_of = [sb(f"head_of{n}", [P, HEADS[n]]) for n in range(2)]
        head_mask = both(sb, "head_mask", [P, Q])
        exponent = sb("exponent", [P, TG])
        ones3 = sb("ones3", [PARTS, P], BF16)
        vectors = sb("vectors", [2 * NVEC, P])
        vcol = sb("vcol", [P, 2 * NVEC])
        w_raw = both(sb, "w_raw", [P, 3 * D])
        w_in = both(sb, "w_in", [P, 3 * D])
        w_emb = both(sb, "w_emb", [P, EC, 2 * D])
        w_out = both(sb, "w_out", [P, D])
        b_rows = both(sb, "b_rows", [PARTS, 3 * D])
        b_rest = both(sb, "b_rest", [PARTS, 2, 3 * D])
        b_part = both(sb, "b_part", [PARTS, PARTS, 3 * D], BF16)
        b_pick = both(sb, "b_pick", [PARTS, 2, 3 * D])
        b_bf = both(sb, "b_bf", [PARTS, 3 * D], BF16)
        lnb3 = both(sb, "lnb3", [P, PARTS])
        kbias = sb("kbias", [P, 2])
        cond_sb = sb("cond_sb", [P, E])
        cond_t = sb("cond_t", [P, E])
        cond_s = sb("cond_s", [P, E])
        condT = sb("condT", [P, EC, B])
        scale1 = both(sb, "scale1", [P, B])
        shift0 = both(sb, "shift0", [P, B])
        film_scale = both(sb, "film_scale", [P, B])
        film_shift = both(sb, "film_shift", [P, B])
        maskf_sb = sb("maskf_sb", [NT, P])
        maski_sb = sb("maski_sb", [NT, P], I32)
        masked1 = sb("masked1", [NT, P])
        kept1 = sb("kept1", [NT, P])
        neg_rest = sb("neg_rest", [NT, 3, P])
        neg_part = sb("neg_part", [NT, PARTS, P], BF16)
        neg_masked = sb("neg_masked", [NT, P], BF16)
        neg_row = [sb("neg_row0", [PARTS, B * T], BF16), sb("neg_row1", [1, B * T], BF16)]
        keep = both(sb, "keep", [P, NT])

        xs = sb("xs", [P, NT, D])
        stats = both(sb, "stats", [P, TG, 6])
        mv = both(sb, "mv", [P, TG, 2])
        mean_rstd_x = both(sb, "mean_rstd_x", [P, TG])
        var_eps = both(sb, "var_eps", [P, TG])
        rstd = both(sb, "rstd", [P, TG])
        z = both(sb, "z", [P, TG, D])
        zT = both(sb, "zT", [P, R])
        k_max = both(sb, "k_max", [P, BG])
        k_maxb = both(sb, "k_maxb", [P, BG])
        ke = both(sb, "ke", [P, BG, T])
        k_sum = both(sb, "k_sum", [P, BG])
        k_rec = both(sb, "k_rec", [P, BG])
        q_max = [sb(f"q_max{n}", [P, TG, HEADS[n]]) for n in range(2)]
        qe = both(sb, "qe", [P, TG, D])
        qT = both(sb, "qT", [P, R])
        compact = both(sb, "compact", [P, TG, D])
        spread = both(sb, "spread", [P, TG, BT, D])
        att = both(sb, "att", [P, BG, Q])
        att_bd = [sb(f"att_bd{n}", [P, BG, D + HEADS[n]]) for n in range(2)]
        q_rec = [sb(f"q_rec{n}", [P, TG, HEADS[n]]) for n in range(2)]
        y = both(sb, "y", [P, TG, D])
        stats2 = both(sb, "stats2", [P, TG, 6])
        mv2 = both(sb, "mv2", [P, TG, 2])
        var_eps2 = both(sb, "var_eps2", [P, TG])
        rstd2 = both(sb, "rstd2", [P, TG])
        mean_rstd = both(sb, "mean_rstd", [P, TG])
        yn = both(sb, "yn", [P, TG, D])
        fs = both(sb, "fs", [P, BG, T])
        fh = both(sb, "fh", [P, BG, T])
        th = both(sb, "th", [P, BG, T])
        gate = both(sb, "gate", [P, BG, T])

        ps = ctx.enter_context(nc.psum_tensor("ps", [P, 8, 512], F32))

        def bank(product, n):
            return ps[:, PRODUCTS[product, n][0], :]

        def tiles(product, n):
            return bank(product, n).rearrange("p (j c) -> p j c", j=TG)

        def batches(product, n):
            return bank(product, n).rearrange("p (b t) -> p b t", t=T)

        def read_out_tiles(n):
            first = PRODUCTS["read_out", n][0]
            return ps[:, first:first + 2, :].rearrange("p a (b m) -> p (a b) m", b=2)

        loaded = {k: sem(f"loaded_{k}") for k in ("cond", "vectors", "w_raw", "b_rows", "w_emb", "w_out", "masks")}
        x_loaded = sem("x_loaded")
        c_ident, c_sel, c_spread, c_pool = sem("c_ident"), sem("c_sel"), sem("c_spread"), sem("c_pool")
        c_ones, c_hmask, c_attbd = sem("c_ones"), sem("c_hmask"), sem("c_attbd")
        c_win, c_wout, c_negp, c_neg, c_kept1 = sem("c_win"), sem("c_wout"), sem("c_negp"), sem("c_neg"), sem("c_kept1")
        c_negrow, c_tr, c_vcol, c_keep = sem("c_negrow"), sem("c_tr"), sem("c_vcol"), sem("c_keep")
        c_tanh, c_silu, c_cT, c_condT = sem("c_tanh"), sem("c_silu"), sem("c_cT"), sem("c_condT")
        c_film_ps, c_film1, c_film = sem("c_film_ps"), sem("c_film1"), sem("c_film")
        c_lnb3, c_bias_ps, c_bstep, c_bias, c_kb = sem("c_lnb3"), sem("c_bias_ps"), sem("c_bstep"), sem("c_bias"), sem("c_kb")

        names = ("x_seen", "stat", "stat_seen", "stat2_seen", "moments", "var_eps", "rstd", "mean_rstd_x", "z", "z_ps", "zT", "k_ps", "q_ps", "v_ps", "k_max", "k_maxb", "k_sub",
                 "k_exp", "k_sum", "k_rec", "k_norm", "kT_ps", "q_max", "q_sub", "q_exp", "qT_ps", "qT", "compact",
                 "spread", "att_ps", "att", "att_seen", "att_bd", "y_ps", "q_rec", "y", "stat2", "moments2", "var_eps2", "rstd2",
                 "mean_rstd", "yn", "ynT_ps", "fs", "fh", "tanh", "gate", "out_ps", "done")
        S = {k: both(sem, f"s_{k}_") for k in names}
        stored = sem("stored")

        def seen(eng, name, n, g, per=1):
            eng.wait_ge(S[name][n], (g + 1) * per)

        def reused(eng, name, n, g, per=1):
            if not isinstance(g, int) or g > 0:
                eng.wait_ge(S[name][n], g * per)

        def run(eng, steps, order):
            first = 1 + max(lag for *_, lag in LAGS)
            for i in range(first):
                for name, n, lag in order:
                    if i - lag >= 0:
                        steps[name](n, i - lag)
            with eng.Fori(first, NG) as i:
                for name, n, lag in order:
                    steps[name](n, i - lag)
            for i in range(NG, NG + first - 1):
                for name, n, lag in order:
                    if i - lag < NG:
                        steps[name](n, i - lag)

        def per_head(ap, n):
            return ap.rearrange("p t (h c) -> p t h c", h=HEADS[n])

        block = ctx.enter_context(nc.Block())

        x_v = x.rearrange("b t c -> (b t) c").rearrange("(j p) c -> p j c", p=P)
        out_v = out.rearrange("b t c -> (b t) c").rearrange("(j p) c -> p j c", p=P)

        @block.sync
        def _(sp):
            sp.dma_start(xs[:, 0:TG, :], x_v[:, 0:TG, :]).then_inc(x_loaded, 16)
            for n in range(2):
                for m, w in enumerate(("Wq", "Wv", "Wk")):
                    sp.dma_start(w_raw[n][:, m * D:(m + 1) * D], layers[n][w]).then_inc(loaded["w_raw"], 16)
            for n in range(2):
                sp.dma_start(w_out[n][:, :], layers[n]["W_out"]).then_inc(loaded["w_out"], 16)
            with sp.Fori(1, NG) as g:
                sp.wait_ge(x_loaded, g * 16)
                sp.dma_start(xs[:, bass.ds(g * TG, TG), :], x_v[:, bass.ds(g * TG, TG), :]).then_inc(x_loaded, 16)
            with sp.Fori(0, NG) as g:
                seen(sp, "done", 1, g)
                sp.dma_start(out_v[:, bass.ds(g * TG, TG), :], xs[:, bass.ds(g * TG, TG), :]).then_inc(stored, 16)
            sp.wait_ge(stored, NG * 16)

        @block.gpsimd
        def _(pool):
            g_ = nc.gpsimd
            for n in range(2):
                for row, v in ((LNW, "ln_w"), (LNB, "ln_b"), (BK, "bk"), (LN2W, "ln2_w"), (LN2B, "ln2_b")):
                    pool.dma_start(vectors[n * NVEC + row:n * NVEC + row + 1, :],
                                   layers[n][v].rearrange("(a c) -> a c", a=1)).then_inc(loaded["vectors"], 16)
                pool.dma_start(vectors[n * NVEC + BSCALE:n * NVEC + BSHIFT + 1, :],
                               layers[n]["b_emb"].rearrange("(a c) -> a c", a=2)).then_inc(loaded["vectors"], 16)
            g_.memset(ident[:, :], 0.0).then_inc(c_pool, 1)
            g_.memset(exponent[:, :], -0.5).then_inc(c_pool, 1)
            for n in range(2):
                g_.memset(head_of[n][:, :], 1.0).then_inc(c_pool, 1)
            pool.wait_ge(c_pool, 4)
            g_.affine_select(out=ident[:, :], in_=ident[:, :], compare_op=ALU.not_equal, fill=1.0, base=0,
                             pattern=[[-1, P]], channel_multiplier=1).then_inc(c_ident, 1)
            for n in range(2):
                w = D // HEADS[n]
                g_.affine_select(out=head_of[n][:, :], in_=head_of[n][:, :], compare_op=ALU.is_ge, fill=0.0, base=0,
                                 pattern=[[-w, HEADS[n]]], channel_multiplier=1).then_inc(c_sel, 1)
            for n in range(2):
                w = D // HEADS[n]
                pool.wait_ge(c_sel, n + 2)
                g_.affine_select(out=head_of[n][:, :], in_=head_of[n][:, :], compare_op=ALU.is_ge, fill=0.0,
                                 base=w - 1, pattern=[[w, HEADS[n]]], channel_multiplier=-1).then_inc(c_sel, 1)
            for n in range(2):
                g_.memset(spread[n][:, :, :, :], 0.0).then_inc(c_spread, 1)
                g_.memset(att_bd[n][:, :, 0:D], 0.0).then_inc(c_attbd, 1)

            def rstd_x(n, g):
                seen(pool, "var_eps", n, g)
                reused(pool, "z", n, g, TG)
                g_.tensor_tensor(rstd[n][:, :], var_eps[n][:, :], exponent[:, :], ALU.pow).then_inc(S["rstd"][n], 1)
                seen(pool, "rstd", n, g)

            def scale_k(n, g):
                seen(pool, "k_rec", n, g)
                g_.tensor_tensor(ke[n][:, :, :], ke[n][:, :, :], k_rec[n][:, :].unsqueeze(2).to_broadcast([P, BG, T]),
                                 ALU.mult).then_inc(S["k_norm"][n], 1)
                seen(pool, "k_norm", n, g)

            def spread_att(n, g):
                reused(pool, "y_ps", n, g)
                seen(pool, "att", n, g)
                pool.sem_inc(S["att_seen"][n], 1)
                for r in range(NQ):
                    part = slice(r * Q, (r + 1) * Q)
                    g_.tensor_scalar(att_bd[n][part, :, r * Q:(r + 1) * Q], att[n][part, :, :], 1.0, 0.0,
                                     ALU.mult, ALU.add).then_inc(S["att_bd"][n], 1)
                seen(pool, "att_bd", n, g, NQ)

            def rstd_y(n, g):
                seen(pool, "var_eps2", n, g)
                reused(pool, "yn", n, g, TG)
                g_.tensor_tensor(rstd2[n][:, :], var_eps2[n][:, :], exponent[:, :], ALU.pow).then_inc(S["rstd2"][n], 1)
                seen(pool, "rstd2", n, g)

            def film_add(n, g):
                reused(pool, "gate", n, g)
                seen(pool, "fs", n, g)
                g_.tensor_tensor(fh[n][:, :, :], fs[n][:, :, :],
                                 film_shift[n][:, bass.ds(g * BG, BG)].unsqueeze(2).to_broadcast([P, BG, T]),
                                 ALU.add).then_inc(S["fh"][n], 1)
                seen(pool, "fh", n, g)

            pool.wait_ge(c_attbd, 2)
            run(pool, {"rstd_x": rstd_x, "scale_k": scale_k, "spread_att": spread_att, "rstd_y": rstd_y,
                       "film_add": film_add}, ORDER["pool"])

        @block.scalar
        def _(act):
            a_ = nc.scalar
            act.dma_start(cond_sb[:, :], cond).then_inc(loaded["cond"], 16)
            act.dma_start(maskf_sb[:, :], mask_f.rearrange("b t a -> (b t a)").rearrange("(j p) -> j p", p=P)).then_inc(loaded["masks"], 16)
            act.dma_start(maski_sb[:, :], mask_i.rearrange("b t -> (b t)").rearrange("(j p) -> j p", p=P)).then_inc(loaded["masks"], 16)
            for n in range(2):
                for m, v in enumerate(("bq", "bv", "b_out")):
                    for i in range(PARTS):
                        act.dma_start(b_rows[n][i:i + 1, m * D:(m + 1) * D],
                                      layers[n][v].rearrange("(a c) -> a c", a=1)).then_inc(loaded["b_rows"], 16)
            for n in range(2):
                act.dma_start(w_emb[n][:, :, :], layers[n]["W_emb"].rearrange("(k p) m -> p k m", p=P)).then_inc(loaded["w_emb"], 16)
            act.wait_ge(loaded["cond"], 16)
            a_.activation(cond_t[:, :], cond_sb[:, :], ACT.Tanh, scale=0.5).then_inc(c_tanh, 1)
            act.wait_ge(c_neg, 4)
            for i in range(PARTS):
                act.dma_start(neg_row[0][i:i + 1, :].rearrange("a (j p) -> a j p", p=P),
                              neg_part[:, i:i + 1, :].rearrange("j a p -> j (a p)")).then_inc(c_negrow, 16)
            act.dma_start(neg_row[1][0:1, :].rearrange("a (j p) -> a j p", p=P), neg_masked[:, :]).then_inc(c_negrow, 16)

            def normalise_x(n, g):
                reused(act, "z_ps", n, g)
                seen(act, "mean_rstd_x", n, g)
                seen(act, "rstd", n, g)
                if n == 0:
                    act.wait_ge(x_loaded, (g + 1) * 16)
                else:
                    seen(act, "done", 0, g)
                for j in range(TG):
                    a_.activation(z[n][:, j, :], xs[:, bass.ds(g * TG + j, 1), :].rearrange("p a c -> p (a c)"),
                                  ACT.Identity, scale=rstd[n][:, j:j + 1], bias=mean_rstd_x[n][:, j:j + 1]
                                  ).then_inc(S["z"][n], 1)

            def copy_zT(n, g):
                for product in ("k_ps", "q_ps", "v_ps"):
                    reused(act, product, n, g)
                seen(act, "z_ps", n, g)
                a_.copy(zT[n][:, :], bank("z_transpose", n)).then_inc(S["zT"][n], 1)

            def exp_k(n, g):
                seen(act, "k_sub", n, g)
                a_.activation(ke[n][:, :, :], ke[n][:, :, :], ACT.Exp).then_inc(S["k_exp"][n], 1)

            def exp_q(n, g):
                seen(act, "q_sub", n, g)
                a_.activation(qe[n][:, :, :], qe[n][:, :, :], ACT.Exp).then_inc(S["q_exp"][n], 1)

            def copy_v(n, g):
                reused(act, "att_ps", n, g)
                seen(act, "v_ps", n, g)
                v = tiles("project_v", n)
                if n == 0:
                    for r in range(NQ):
                        part = slice(r * Q, (r + 1) * Q)
                        a_.copy(spread[0][part, :, r, :], v[part, :, :]).then_inc(S["spread"][0], 1)
                else:
                    for j in range(TG):
                        a_.activation(compact[1][:, j, :], v[:, j, :], ACT.Copy,
                                      scale=keep[1][:, bass.ds(g * TG + j, 1)]).then_inc(S["compact"][1], 1)

            def copy_k(n, g):
                reused(act, "att_ps", n, g)
                seen(act, "kT_ps", n, g)
                k = tiles("k_transpose", n)
                if n == 0:
                    for j in range(TG):
                        a_.activation(compact[0][:, j, :], k[:, j, :], ACT.Copy,
                                      scale=keep[0][:, bass.ds(g * TG + j, 1)]).then_inc(S["compact"][0], 1)
                else:
                    for r in range(NQ):
                        part = slice(r * Q, (r + 1) * Q)
                        a_.copy(spread[1][part, :, r, :], k[part, :, :]).then_inc(S["spread"][1], 1)

            def copy_qT(n, g):
                reused(act, "y_ps", n, g)
                seen(act, "qT_ps", n, g)
                a_.copy(qT[n][:, :], bank("q_transpose", n)).then_inc(S["qT"][n], 1)

            def normalise_y(n, g):
                reused(act, "ynT_ps", n, g)
                seen(act, "mean_rstd", n, g)
                seen(act, "rstd2", n, g)
                seen(act, "y", n, g)
                for j in range(TG):
                    a_.activation(yn[n][:, j, :], y[n][:, j, :], ACT.Identity, scale=rstd2[n][:, j:j + 1],
                                  bias=mean_rstd[n][:, j:j + 1]).then_inc(S["yn"][n], 1)

            def tanh_h(n, g):
                reused(act, "gate", n, g)
                seen(act, "fh", n, g)
                a_.activation(th[n][:, :, :], fh[n][:, :, :], ACT.Tanh, scale=0.5).then_inc(S["tanh"][n], 1)

            act.wait_ge(c_spread, 2)
            act.wait_ge(c_keep, 2)
            run(act, {"normalise_x": normalise_x, "copy_zT": copy_zT, "copy_v": copy_v, "exp_k": exp_k, "exp_q": exp_q,
                      "copy_qT": copy_qT, "copy_k": copy_k, "normalise_y": normalise_y, "tanh_h": tanh_h},
                ORDER["scalar"])

        @block.vector
        def _(dve):
            v_ = nc.vector
            v_.memset(ones3[:, :], 1.0).then_inc(c_ones, 1)

            def x_stats(n, g):
                reused(dve, "rstd", n, g)
                if n == 0:
                    dve.wait_ge(x_loaded, (g + 1) * 16)
                else:
                    seen(dve, "done", 0, g)
                dve.sem_inc(S["x_seen"][n], 1)
                for j in range(TG):
                    v_.bn_stats(stats[n][:, j, :], xs[:, bass.ds(g * TG + j, 1), :].rearrange("p a c -> p (a c)")
                                ).then_inc(S["stat"][n], 1)
                seen(dve, "stat", n, g, TG)
                dve.sem_inc(S["stat_seen"][n], 1)
                for j in range(TG):
                    v_.bn_aggr(mv[n][:, j, :], stats[n][:, j, :]).then_inc(S["moments"][n], 1)
                seen(dve, "moments", n, g, TG)
                v_.tensor_scalar(var_eps[n][:, :], mv[n][:, :, 1], EPS, None, ALU.add).then_inc(S["var_eps"][n], 1)

            def mean_rstd_x_(n, g):
                reused(dve, "z", n, g, TG)
                seen(dve, "rstd", n, g)
                v_.scalar_tensor_tensor(mean_rstd_x[n][:, :], mv[n][:, :, 0], -1.0, rstd[n][:, :], ALU.mult, ALU.mult
                                        ).then_inc(S["mean_rstd_x"][n], 1)

            def k_softmax_in(n, g):
                seen(dve, "k_ps", n, g)
                k = batches("project_k", n)
                v_.tensor_reduce(k_max[n][:, :], k, X, ALU.max).then_inc(S["k_max"][n], 1)
                seen(dve, "k_max", n, g)
                v_.tensor_scalar(k_maxb[n][:, :], k_max[n][:, :], kbias[:, n:n + 1], None, ALU.add
                                 ).then_inc(S["k_maxb"][n], 1)
                seen(dve, "k_maxb", n, g)
                reused(dve, "kT_ps", n, g)
                v_.scalar_tensor_tensor(ke[n][:, :, :], k, kbias[:, n:n + 1],
                                        k_maxb[n][:, :].unsqueeze(2).to_broadcast([P, BG, T]),
                                        ALU.add, ALU.subtract).then_inc(S["k_sub"][n], 1)

            def q_softmax_in(n, g):
                seen(dve, "q_ps", n, g)
                q = per_head(tiles("project_q", n), n)
                v_.tensor_reduce(q_max[n][:, :, :], q, X, ALU.max).then_inc(S["q_max"][n], 1)
                seen(dve, "q_max", n, g)
                reused(dve, "qT_ps", n, g)
                v_.tensor_tensor(per_head(qe[n][:, :, :], n), q,
                                 q_max[n][:, :, :].unsqueeze(3).to_broadcast([P, TG, HEADS[n], D // HEADS[n]]),
                                 ALU.subtract).then_inc(S["q_sub"][n], 1)

            def k_sums(n, g):
                reused(dve, "k_norm", n, g)
                seen(dve, "k_exp", n, g)
                v_.tensor_reduce(k_sum[n][:, :], ke[n][:, :, :], X, ALU.add).then_inc(S["k_sum"][n], 1)
                seen(dve, "k_sum", n, g)
                v_.reciprocal(k_rec[n][:, :], k_sum[n][:, :]).then_inc(S["k_rec"][n], 1)

            def mask_att(n, g):
                reused(dve, "att_bd", n, g, NQ)
                seen(dve, "att_ps", n, g)
                v_.tensor_tensor(att[n][:, :, :], batches("attend", n),
                                 head_mask[n][:, :].unsqueeze(1).to_broadcast([P, BG, Q]), ALU.mult
                                 ).then_inc(S["att"][n], 1)

            def y_div(n, g):
                wide = read_out_tiles(n)
                reused(dve, "yn", n, g, TG)
                seen(dve, "y_ps", n, g)
                v_.reciprocal(q_rec[n][:, :, :], wide[:, :, D:D + HEADS[n]]).then_inc(S["q_rec"][n], 1)
                seen(dve, "q_rec", n, g)
                v_.tensor_tensor(per_head(y[n][:, :, :], n), per_head(wide[:, :, 0:D], n),
                                 q_rec[n][:, :, :].unsqueeze(3).to_broadcast([P, TG, HEADS[n], D // HEADS[n]]),
                                 ALU.mult).then_inc(S["y"][n], 1)

            def y_stats(n, g):
                reused(dve, "rstd2", n, g)
                seen(dve, "y", n, g)
                for j in range(TG):
                    v_.bn_stats(stats2[n][:, j, :], y[n][:, j, :]).then_inc(S["stat2"][n], 1)
                seen(dve, "stat2", n, g, TG)
                dve.sem_inc(S["stat2_seen"][n], 1)
                for j in range(TG):
                    v_.bn_aggr(mv2[n][:, j, :], stats2[n][:, j, :]).then_inc(S["moments2"][n], 1)
                seen(dve, "moments2", n, g, TG)
                v_.tensor_scalar(var_eps2[n][:, :], mv2[n][:, :, 1], EPS, None, ALU.add).then_inc(S["var_eps2"][n], 1)

            def mean_rstd_y(n, g):
                reused(dve, "yn", n, g, TG)
                seen(dve, "rstd2", n, g)
                v_.scalar_tensor_tensor(mean_rstd[n][:, :], mv2[n][:, :, 0], -1.0, rstd2[n][:, :], ALU.mult, ALU.mult
                                        ).then_inc(S["mean_rstd"][n], 1)

            def film_mul(n, g):
                reused(dve, "fh", n, g)
                seen(dve, "ynT_ps", n, g)
                v_.tensor_tensor(fs[n][:, :, :], batches("y_transpose", n),
                                 film_scale[n][:, bass.ds(g * BG, BG)].unsqueeze(2).to_broadcast([P, BG, T]),
                                 ALU.mult).then_inc(S["fs"][n], 1)

            def gate_h(n, g):
                reused(dve, "out_ps", n, g)
                seen(dve, "tanh", n, g)
                seen(dve, "fh", n, g)
                v_.scalar_tensor_tensor(gate[n][:, :, :], th[n][:, :, :], 1.0, fh[n][:, :, :], ALU.add, ALU.mult
                                        ).then_inc(S["gate"][n], 1)

            def residual(n, g):
                seen(dve, "out_ps", n, g)
                rows = xs[:, bass.ds(g * TG, TG), :]
                v_.tensor_tensor(rows, tiles("project_out", n), rows, ALU.add
                                 ).then_inc(S["done"][n], 1)

            def setup_weights():
                dve.wait_ge(c_vcol, 1)
                dve.wait_ge(loaded["w_raw"], 6 * 16)
                dve.wait_ge(loaded["w_out"], 2 * 16)
                for n in range(2):
                    v_.tensor_copy(lnb3[n][:, :], vcol[:, n * NVEC + LNB:n * NVEC + LNB + 1].to_broadcast([P, PARTS])
                                   ).then_inc(c_lnb3, 1)
                for n in range(2):
                    v_.tensor_scalar(w_in[n][:, :], w_raw[n][:, :], vcol[:, n * NVEC + LNW:n * NVEC + LNW + 1], None,
                                     ALU.mult).then_inc(c_win, 1)
                    v_.tensor_scalar(w_out[n][:, :], w_out[n][:, :], 0.5, None, ALU.mult).then_inc(c_wout, 1)

            def setup_masks():
                dve.wait_ge(loaded["masks"], 2 * 16)
                v_.tensor_scalar(neg_rest[:, 0, :], maskf_sb[:, :], -1.0, 1000000.0, ALU.add, ALU.mult).then_inc(c_negp, 1)
                v_.tensor_scalar(masked1[:, :], maski_sb[:, :], 1.0, None, ALU.is_equal).then_inc(c_negp, 1)
                dve.wait_ge(c_negp, 2)
                v_.tensor_scalar(kept1[:, :], masked1[:, :], -1.0, 1.0, ALU.mult, ALU.add).then_inc(c_kept1, 1)
                v_.tensor_scalar(neg_masked[:, :], masked1[:, :], -1e30, None, ALU.mult).then_inc(c_neg, 1)
                v_.tensor_copy(neg_part[:, 0, :], neg_rest[:, 0, :]).then_inc(c_neg, 1)
                for i in (1, 2):
                    dve.wait_ge(c_neg, i + 1)
                    v_.tensor_tensor(neg_rest[:, i, :], neg_rest[:, i - 1, :], neg_part[:, i - 1, :], ALU.subtract
                                     ).then_inc(c_negp, 1)
                    dve.wait_ge(c_negp, 2 + i)
                    v_.tensor_copy(neg_part[:, i, :], neg_rest[:, i, :]).then_inc(c_neg, 1)

            def setup_columns():
                dve.wait_ge(c_tr, 1)
                v_.tensor_copy(vcol[:, :], ps[:, 0, 0:2 * NVEC]).then_inc(c_vcol, 1)
                for n in range(2):
                    v_.tensor_copy(keep[n][:, :], ps[:, 0, 32 + n * NT:32 + (n + 1) * NT]).then_inc(c_keep, 1)
                dve.wait_ge(c_sel, 4)
                for n in range(2):
                    w = D // HEADS[n]
                    for r in range(NQ):
                        part = slice(r * Q, (r + 1) * Q)
                        hs = head_of[n][part, r * Q // w:(r + 1) * Q // w]
                        v_.tensor_copy(head_mask[n][part, :].rearrange("p (h c) -> p h c", c=w),
                                       hs.unsqueeze(2).to_broadcast([Q, Q // w, w])).then_inc(c_hmask, 1)
                    v_.tensor_copy(att_bd[n][:, :, D:D + HEADS[n]],
                                   head_of[n][:, :].unsqueeze(1).to_broadcast([P, BG, HEADS[n]])).then_inc(c_hmask, 1)

            def setup_biases():
                dve.wait_ge(c_bias_ps, 1)
                dve.wait_ge(loaded["b_rows"], 2 * 9 * 16)
                for n in range(2):
                    v_.tensor_tensor(b_rest[n][:, 0, 0:2 * D], ps[0:PARTS, 1, n * 2 * D:(n + 1) * 2 * D],
                                     b_rows[n][:, 0:2 * D], ALU.add).then_inc(c_bstep, 1)
                    v_.tensor_copy(b_rest[n][:, 0, 2 * D:3 * D], b_rows[n][:, 2 * D:3 * D]).then_inc(c_bstep, 1)
                    v_.tensor_scalar(kbias[:, n:n + 1], ps[:, 2, n:n + 1], vcol[:, n * NVEC + BK:n * NVEC + BK + 1],
                                     None, ALU.add).then_inc(c_kb, 1)
                dve.wait_ge(c_bstep, 4)
                count = 4
                for n in range(2):
                    v_.tensor_copy(b_part[n][:, 0, :], b_rest[n][:, 0, :]).then_inc(c_bstep, 1)
                    count += 1
                    for src, dst, i in ((0, 1, 1), (1, 0, 2)):
                        dve.wait_ge(c_bstep, count)
                        v_.tensor_tensor(b_rest[n][:, dst, :], b_rest[n][:, src, :], b_part[n][:, i - 1, :], ALU.subtract
                                         ).then_inc(c_bstep, 1)
                        dve.wait_ge(c_bstep, count + 1)
                        v_.tensor_copy(b_part[n][:, i, :], b_rest[n][:, dst, :]).then_inc(c_bstep, 1)
                        count += 2
                    dve.wait_ge(c_bstep, count)
                    v_.tensor_scalar(b_pick[n][:, 0, :], b_part[n][:, 0, :], ident[0:PARTS, 0:1], None, ALU.mult
                                     ).then_inc(c_bstep, 1)
                    dve.wait_ge(c_bstep, count + 1)
                    v_.scalar_tensor_tensor(b_pick[n][:, 1, :], b_part[n][:, 1, :], ident[0:PARTS, 1:2],
                                            b_pick[n][:, 0, :], ALU.mult, ALU.add).then_inc(c_bstep, 1)
                    dve.wait_ge(c_bstep, count + 2)
                    v_.scalar_tensor_tensor(b_bf[n][:, :], b_part[n][:, 2, :], ident[0:PARTS, 2:3],
                                            b_pick[n][:, 1, :], ALU.mult, ALU.add).then_inc(c_bias, 1)
                    count += 2

            def setup_silu():
                dve.wait_ge(c_tanh, 1)
                v_.scalar_tensor_tensor(cond_s[:, :], cond_t[:, :], 1.0, cond_sb[:, :], ALU.add, ALU.mult
                                        ).then_inc(c_silu, 1)
                dve.wait_ge(c_cT, 1)
                v_.tensor_scalar(condT[:, :, :], ps[:, 0, 128:128 + EC * B].rearrange("p (k b) -> p k b", k=EC), 0.5,
                                 None, ALU.mult).then_inc(c_condT, 1)

            def setup_film():
                dve.wait_ge(c_film_ps, 1)
                for n in range(2):
                    col = n * NVEC
                    v_.tensor_scalar(scale1[n][:, :], ps[:, 3, 2 * n * B:(2 * n + 1) * B],
                                     vcol[:, col + BSCALE:col + BSCALE + 1], 1.0, ALU.add, ALU.add).then_inc(c_film1, 1)
                    v_.tensor_scalar(shift0[n][:, :], ps[:, 3, (2 * n + 1) * B:(2 * n + 2) * B],
                                     vcol[:, col + BSHIFT:col + BSHIFT + 1], None, ALU.add).then_inc(c_film1, 1)
                dve.wait_ge(c_film1, 4)
                for n in range(2):
                    col = n * NVEC
                    v_.tensor_scalar(film_scale[n][:, :], scale1[n][:, :], vcol[:, col + LN2W:col + LN2W + 1], None,
                                     ALU.mult).then_inc(c_film, 1)
                    v_.scalar_tensor_tensor(film_shift[n][:, :], scale1[n][:, :], vcol[:, col + LN2B:col + LN2B + 1],
                                            shift0[n][:, :], ALU.mult, ALU.add).then_inc(c_film, 1)

            setup_masks()
            setup_columns()
            setup_weights()
            setup_biases()
            setup_silu()
            setup_film()
            dve.wait_ge(c_kb, 2)
            dve.wait_ge(c_hmask, 2 * NQ + 2)
            dve.wait_ge(c_film, 4)
            run(dve, {"x_stats": x_stats, "mean_rstd_x": mean_rstd_x_, "k_in": k_softmax_in, "q_in": q_softmax_in,
                      "k_sums": k_sums, "mask_att": mask_att, "y_div": y_div, "y_stats": y_stats,
                      "mean_rstd": mean_rstd_y, "film_mul": film_mul, "gate_h": gate_h, "residual": residual},
                ORDER["vector"])

        @block.tensor
        def _(pe):
            t_ = nc.tensor

            def transpose_rows(src, dst):
                for j in range(TG):
                    last = t_.transpose(dst[:, j * P:(j + 1) * P], src[:, j, :], ident[:, :])
                return last

            def bank_free(product, n, g):
                before = PRODUCTS[product, n][1]
                for name, m, later, per in before:
                    group = g + later
                    if isinstance(g, int):
                        group = min(group, NG - 1)
                        if group < 0:
                            continue
                    seen(pe, name, m, group, per)

            def z_transpose(n, g):
                bank_free("z_transpose", n, g)
                seen(pe, "z", n, g, TG)
                transpose_rows(z[n], bank("z_transpose", n)).then_inc(S["z_ps"][n], 1)

            def project_k(n, g):
                bank_free("project_k", n, g)
                seen(pe, "zT", n, g)
                t_.matmul(bank("project_k", n), w_in[n][:, 2 * D:3 * D], zT[n][:, :], start=True, stop=False)
                parts = PARTS if n == 0 else 1
                t_.matmul(bank("project_k", n), ones3[0:parts, :], neg_row[n][0:parts, bass.ds(g * R, R)], start=False,
                          stop=True).then_inc(S["k_ps"][n], 1)

            def project_rows(product, n, m):
                t_.matmul(bank(product, n), ones3[:, :],
                          b_bf[n][:, m * D:(m + 1) * D].unsqueeze(1).to_broadcast([PARTS, TG, D]), start=True, stop=False)
                for j in range(TG):
                    last = t_.matmul(bank(product, n)[:, j * D:(j + 1) * D], zT[n][:, j * P:(j + 1) * P],
                                     w_in[n][:, m * D:(m + 1) * D], start=False, stop=j == TG - 1)
                return last

            def project_q(n, g):
                bank_free("project_q", n, g)
                seen(pe, "zT", n, g)
                project_rows("project_q", n, 0).then_inc(S["q_ps"][n], 1)

            def project_v(n, g):
                bank_free("project_v", n, g)
                seen(pe, "zT", n, g)
                project_rows("project_v", n, 1).then_inc(S["v_ps"][n], 1)

            def k_transpose(n, g):
                bank_free("k_transpose", n, g)
                seen(pe, "k_norm", n, g)
                transpose_rows(ke[n][:, :, :].rearrange("p (j b) t -> p j (b t)", j=TG), bank("k_transpose", n)
                               ).then_inc(S["kT_ps"][n], 1)

            def q_transpose(n, g):
                bank_free("q_transpose", n, g)
                seen(pe, "q_exp", n, g)
                transpose_rows(qe[n], bank("q_transpose", n)).then_inc(S["qT_ps"][n], 1)

            def attend(n, g):
                bank_free("attend", n, g)
                seen(pe, "compact", n, g, TG)
                seen(pe, "spread", n, g, NQ)
                for j in range(TG):
                    for r in range(NQ):
                        last = t_.matmul(ps[r * Q:(r + 1) * Q, PRODUCTS["attend", n][0], j * P:(j + 1) * P],
                                         compact[n][:, j, r * Q:(r + 1) * Q], spread[n][:, j, :, r * Q:(r + 1) * Q],
                                         start=True, stop=True, tile_position=(0, r * Q))
                last.then_inc(S["att_ps"][n], 1)

            def read_out(n, g):
                bank_free("read_out", n, g)
                wide = read_out_tiles(n)
                seen(pe, "att_bd", n, g, NQ)
                seen(pe, "qT", n, g)
                for b in range(BG):
                    j, r = b // BT, b % BT
                    last = t_.matmul(wide[r * T:(r + 1) * T, j, 0:D + HEADS[n]], qT[n][:, b * T:(b + 1) * T],
                                     att_bd[n][:, b, :], start=True, stop=True, tile_position=(0, r * T))
                last.then_inc(S["y_ps"][n], 1)

            def y_transpose(n, g):
                bank_free("y_transpose", n, g)
                seen(pe, "yn", n, g, TG)
                transpose_rows(yn[n], bank("y_transpose", n)).then_inc(S["ynT_ps"][n], 1)

            def project_out(n, g):
                bank_free("project_out", n, g)
                seen(pe, "gate", n, g)
                h = gate[n][:, :, :].rearrange("p (j b) t -> p j (b t)", j=TG)
                t_.matmul(bank("project_out", n), ones3[:, :],
                          b_bf[n][:, 2 * D:3 * D].unsqueeze(1).to_broadcast([PARTS, TG, D]), start=True, stop=False)
                for j in range(TG):
                    last = t_.matmul(bank("project_out", n)[:, j * P:(j + 1) * P], h[:, j, :], w_out[n][:, :], start=False,
                                     stop=j == TG - 1)
                last.then_inc(S["out_ps"][n], 1)

            pe.wait_ge(c_ident, 1)
            pe.wait_ge(loaded["vectors"], 12 * 16)
            pe.wait_ge(loaded["masks"], 2 * 16)
            pe.wait_ge(c_kept1, 1)
            t_.transpose(ps[:, 0, 0:2 * NVEC], vectors[:, :], ident[0:2 * NVEC, 0:2 * NVEC])
            t_.transpose(ps[:, 0, 32:32 + NT], maskf_sb[:, :], ident[0:NT, 0:NT])
            t_.transpose(ps[:, 0, 32 + NT:32 + 2 * NT], kept1[:, :], ident[0:NT, 0:NT]).then_inc(c_tr, 1)
            pe.wait_ge(c_lnb3, 2)
            for n in range(2):
                t_.matmul(ps[0:PARTS, 1, n * 2 * D:(n + 1) * 2 * D], lnb3[n][:, :], w_raw[n][:, 0:2 * D],
                          start=True, stop=True)
            for n in range(2):
                last = t_.matmul(ps[:, 2, n:n + 1], w_raw[n][:, 2 * D:3 * D], lnb3[n][:, 0:1], start=True, stop=True)
            last.then_inc(c_bias_ps, 1)
            pe.wait_ge(c_silu, 1)
            pe.wait_ge(c_keep, 2)
            for k in range(EC):
                last = t_.transpose(ps[:, 0, 128 + k * B:128 + (k + 1) * B], cond_s[:, k * P:(k + 1) * P], ident[:, :])
            last.then_inc(c_cT, 1)
            pe.wait_ge(c_condT, 1)
            pe.wait_ge(loaded["w_emb"], 2 * 16)
            for n in range(2):
                for half in range(2):
                    for k in range(EC):
                        last = t_.matmul(ps[:, 3, (2 * n + half) * B:(2 * n + half + 1) * B],
                                         w_emb[n][:, k, half * D:(half + 1) * D], condT[:, k, :],
                                         start=(k == 0), stop=(k == EC - 1))
            last.then_inc(c_film_ps, 1)
            pe.wait_ge(c_win, 2)
            pe.wait_ge(c_bias, 2)
            pe.wait_ge(c_negrow, 4 * 16)
            pe.wait_ge(c_hmask, 2 * NQ + 2)
            pe.wait_ge(c_wout, 2)
            pe.wait_ge(c_film, 4)
            run(pe, {"z_transpose": z_transpose, "project_k": project_k, "project_q": project_q,
                     "project_v": project_v, "q_transpose": q_transpose, "k_transpose": k_transpose,
                     "attend": attend, "read_out": read_out, "y_transpose": y_transpose,
                     "project_out": project_out}, ORDER["tensor"])


_L0 = {"ln_w": "L0_cond_ln_w", "ln_b": "L0_cond_ln_b", "Wq": "L0_cond_Wq", "bq": "L0_cond_bq", "Wk": "L0_cond_Wk",
       "bk": "L0_cond_bk", "Wv": "L0_cond_Wv", "bv": "L0_cond_bv", "W_emb": "L0_cond_W_emb", "b_emb": "L0_cond_b_emb",
       "ln2_w": "L0_cond_ln2_w", "ln2_b": "L0_cond_ln2_b", "W_out": "L0_cond_W_out", "b_out": "L0_cond_b_out"}
_L1 = {"ln_w": "L1_cond_norm_scale", "ln_b": "L1_cond_norm_bias", "Wq": "L1_cond_Wq", "bq": "L1_cond_bq",
       "Wk": "L1_cond_Wk", "bk": "L1_cond_bk", "Wv": "L1_cond_Wv", "bv": "L1_cond_bv", "W_emb": "L1_cond_film_emb_W",
       "b_emb": "L1_cond_film_emb_b", "ln2_w": "L1_cond_film_norm_scale", "ln2_b": "L1_cond_film_norm_bias",
       "W_out": "L1_cond_film_out_W", "b_out": "L1_cond_film_out_b"}


def kernel(**inputs):
    import numpy as np
    import concourse.bacc as bacc
    from concourse.bass_utils import run_bass_kernel_spmd

    nc = bacc.Bacc("TRN2", target_bir_lowering=False, num_devices=1)
    arrays, aps = {}, {}
    for name in ["x", "cond_2048", "mask_BxSx1_fk1", "mask_BxS_ik0", *_L0.values(), *_L1.values()]:
        a = np.ascontiguousarray(inputs[name])
        arrays[f"in_{name}"] = a
        aps[name] = nc.dram_tensor(f"in_{name}", a.shape, mybir.dt.from_np(a.dtype), kind="ExternalInput").ap()
    out = nc.dram_tensor("out_0", (B, T, D), F32, kind="ExternalOutput").ap()
    layers = [{k: aps[v] for k, v in names.items()} for names in (_L0, _L1)]
    build(nc, aps["x"], aps["cond_2048"], aps["mask_BxSx1_fk1"], aps["mask_BxS_ik0"], layers, out)
    r = run_bass_kernel_spmd(nc, [arrays], core_ids=[0])
    return r.results[0]["out_0"]
```

```python
from contextlib import ExitStack

import concourse.bass as bass
from concourse import mybir

F32 = mybir.dt.float32
BF16 = mybir.dt.bfloat16
I32 = mybir.dt.int32
ALU = mybir.AluOpType
ACT = mybir.ActivationFunctionType
X = mybir.AxisListType.X

P = 128
B, T, D = 128, 32, 128
E = 256
EC = E // P
NT = B * T // P
TG = 4
NG = NT // TG
BT = P // T
BG = BT * TG
R = TG * P
Q = 32
NQ = P // Q
HEADS = (8, 16)
EPS = 1e-5
PARTS = 3

KP = (2 * PARTS, PARTS + 1)

LNW, LNB, BSCALE, BSHIFT, LN2W, LN2B = range(6)
NVEC = 6
TWO_ONES = 1 + 127 / 2 ** 16


ORDER = {
    "tensor": (
        ("z_transpose", 1, 9),
        ("project_out", 0, 5),
        ("z_transpose", 0, 0),
        ("k_transpose", 1, 10),
        ("project_out", 1, 14),
        ("y_transpose", 0, 4),
        ("project_q", 0, 1),
        ("project_k", 1, 9),
        ("k_transpose", 0, 1),
        ("project_q", 1, 9),
        ("read_out", 1, 11),
        ("attend", 1, 10),
        ("q_transpose", 0, 2),
        ("project_k", 0, 0),
        ("q_transpose", 1, 10),
        ("project_v", 0, 0),
        ("attend", 0, 1),
        ("y_transpose", 1, 12),
        ("project_v", 1, 9),
        ("read_out", 0, 2),
    ),
    "scalar": (
        ("normalise_x", 0, 0),
        ("exp_k", 1, 10),
        ("normalise_x", 1, 9),
        ("tanh_h", 1, 14),
        ("exp_k", 0, 1),
        ("copy_qT", 1, 11),
        ("normalise_y", 0, 4),
        ("exp_q", 0, 2),
        ("copy_zT", 1, 9),
        ("copy_v", 1, 10),
        ("copy_k", 1, 10),
        ("copy_v", 0, 1),
        ("exp_q", 1, 10),
        ("copy_zT", 0, 0),
        ("copy_k", 0, 1),
        ("tanh_h", 0, 4),
        ("normalise_y", 1, 12),
        ("copy_qT", 0, 2),
    ),
    "vector": (
        ("x_bn", 0, 0),
        ("x_aggr", 0, 0),
        ("film_mul", 0, 5),
        ("x_aggr", 1, 9),
        ("x_eps", 0, 0),
        ("q_max", 0, 2),
        ("k_max", 1, 10),
        ("x_eps", 1, 9),
        ("k_sub", 1, 10),
        ("y_bn", 0, 4),
        ("y_aggr", 0, 4),
        ("q_rec", 1, 12),
        ("y_eps", 0, 4),
        ("k_sum", 1, 10),
        ("k_max", 0, 1),
        ("k_sub", 0, 1),
        ("gate_h", 0, 5),
        ("k_rec", 1, 10),
        ("y_mul", 1, 12),
        ("mask_att", 1, 11),
        ("gate_h", 1, 14),
        ("y_bn", 1, 12),
        ("q_sub", 0, 2),
        ("k_sum", 0, 1),
        ("q_max", 1, 10),
        ("k_rec", 0, 1),
        ("y_aggr", 1, 12),
        ("mask_att", 0, 2),
        ("q_rec", 0, 3),
        ("q_sub", 1, 10),
        ("y_mul", 0, 3),
        ("y_eps", 1, 12),
        ("film_mul", 1, 13),
        ("residual", 1, 14),
        ("residual", 0, 5),
        ("x_bn", 1, 8),
    ),
    "pool": (
        ("rstd_x", 1, 9),
        ("rstd_x", 0, 0),
        ("rstd_y", 0, 4),
        ("scale_k", 0, 1),
        ("scale_k", 1, 10),
        ("spread_att", 0, 2),
        ("spread_att", 1, 11),
        ("rstd_y", 1, 12),
        ("film_add", 0, 4),
        ("film_add", 1, 13),
    ),
}
LAGS = [entry for order in ORDER.values() for entry in order]
LOOPS = [(1 + max(lag for _, m, lag in LAGS if m == n), NG + min(lag for _, m, lag in LAGS if m == n)) for n in range(2)]
PRODUCTS = {
    ("z_transpose", 0): (2, (("zT", 1, -9, 1), ("k_sub", 1, -10, 1), ("zT", 0, -1, 1),)),
    ("project_k", 0): (6, (("done", 1, -14, 1), ("y", 0, -3, 1), ("qT", 1, -11, 1), ("k_sub", 0, -1, 1),)),
    ("project_q", 0): (1, (("q_sub", 1, -9, 1), ("q_sub", 0, -1, 1),)),
    ("project_v", 0): (3, (("att", 1, -10, 1), ("spread", 1, -10, 4), ("spread", 0, -1, 4),)),
    ("q_transpose", 0): (5, (("y", 1, -9, 1), ("done", 0, -3, 1), ("qT", 0, -1, 1),)),
    ("k_transpose", 0): (7, (("y", 0, -2, 1), ("fs", 1, -12, 1), ("compact", 0, -1, 4),)),
    ("attend", 0): (0, (("compact", 1, -9, 4), ("att", 0, -1, 1),)),
    ("read_out", 0): (6, (("fs", 1, -10, 1), ("qT", 1, -8, 1), ("k_sub", 0, 2, 1), ("compact", 0, 1, 4), ("done", 1, -12, 1), ("y", 0, -1, 1),)),
    ("y_transpose", 0): (4, (("y", 1, -8, 1), ("fs", 0, -1, 1),)),
    ("project_out", 0): (5, (("qT", 0, 2, 1), ("y", 1, -7, 1), ("done", 0, -1, 1),)),
    ("z_transpose", 1): (2, (("k_sub", 1, -1, 1), ("zT", 0, 8, 1), ("zT", 1, -1, 1),)),
    ("project_k", 1): (2, (("zT", 0, 9, 1), ("zT", 1, 0, 1), ("k_sub", 1, -1, 1),)),
    ("project_q", 1): (1, (("q_sub", 0, 8, 1), ("q_sub", 1, -1, 1),)),
    ("project_v", 1): (0, (("att", 0, 8, 1), ("compact", 1, -1, 4),)),
    ("q_transpose", 1): (6, (("k_sub", 0, 10, 1), ("done", 1, -4, 1), ("y", 0, 7, 1), ("qT", 1, -1, 1),)),
    ("k_transpose", 1): (3, (("spread", 0, 9, 4), ("att", 1, -1, 1), ("spread", 1, -1, 4),)),
    ("attend", 1): (3, (("spread", 1, 0, 4), ("spread", 0, 9, 4), ("att", 1, -1, 1),)),
    ("read_out", 1): (4, (("fs", 0, 7, 1), ("done", 0, 6, 1), ("qT", 0, 8, 1), ("y", 1, -1, 1),)),
    ("y_transpose", 1): (7, (("compact", 0, 11, 4), ("y", 0, 9, 1), ("fs", 1, -1, 1),)),
    ("project_out", 1): (6, (("y", 0, 11, 1), ("qT", 1, 3, 1), ("k_sub", 0, 13, 1), ("done", 1, -1, 1),)),
}
SETUP_BANK, COND_BANK, MASK_BANK = 4, 5, 7


def build(nc, x, cond, mask_f, mask_i, layers, out):
    ctx = ExitStack()
    with ctx:
        def sb(name, shape, dt=F32):
            return ctx.enter_context(nc.sbuf_tensor(name, shape, dt))

        def both(make, name, *args):
            return [make(f"{name}{n}", *args) for n in range(2)]

        def sem(name):
            return ctx.enter_context(nc.semaphore(name))

        ident = sb("ident", [P, P])
        head_of = [sb(f"head_of{n}", [P, HEADS[n]]) for n in range(2)]
        head_mask = both(sb, "head_mask", [P, Q])
        exponent = sb("exponent", [P, TG])
        ones3 = sb("ones3", [PARTS, P], BF16)
        vectors = both(sb, "vectors", [NVEC, P])
        vcol = both(sb, "vcol", [P, NVEC])
        w_raw = both(sb, "w_raw", [P, 3 * D])
        w_in = both(sb, "w_in", [P, 3 * D])
        w_emb = both(sb, "w_emb", [P, EC, 2 * D])
        w_out = both(sb, "w_out", [P, D])
        lnb_cols = both(sb, "lnb_cols", [P, PARTS])
        later_parts = sb("later_parts", [PARTS, 2])
        bias = both(sb, "bias", [PARTS, 4 * D])
        b_rest = both(sb, "b_rest", [PARTS, 2, 4 * D])
        b_part = both(sb, "b_part", [PARTS, 2, 4 * D], BF16)
        b_bf = both(sb, "b_bf", [KP[0], 4 * D], BF16)
        cond_sb = sb("cond_sb", [P, E])
        cond_t = sb("cond_t", [P, E])
        cond_s = sb("cond_s", [P, E])
        condT = sb("condT", [P, EC, B])
        scale1 = both(sb, "scale1", [P, B])
        shift0 = both(sb, "shift0", [P, B])
        film_scale = both(sb, "film_scale", [P, B])
        film_shift = both(sb, "film_shift", [P, B])
        maskf_sb = sb("maskf_sb", [NT, P])
        maski_sb = sb("maski_sb", [NT, P], I32)
        masked1 = sb("masked1", [NT, P])
        kept1 = sb("kept1", [NT, P])
        any_kept = sb("any_kept", [NT, BT])
        any_diagonal = sb("any_diagonal", [NT, NT, BT])
        ones_tiles = sb("ones_tiles", [NT, P])
        any_batch = sb("any_batch", [P, B])
        any_rec = sb("any_rec", [P, B])
        one_or_nan = sb("one_or_nan", [P, B])
        film_plain1 = sb("film_plain1", [P, B])
        neg_rest = sb("neg_rest", [NT, 3, P])
        neg_part = sb("neg_part", [NT, PARTS, P], BF16)
        neg_masked = sb("neg_masked", [NT, P], BF16)
        neg_row = both(sb, "neg_row", [KP[0], B * T], BF16)
        keep = both(sb, "keep", [P, NT])

        xs = sb("xs", [P, NT, D])
        stats = both(sb, "stats", [P, TG, 6])
        mv = both(sb, "mv", [P, TG, 2])
        neg_mean = both(sb, "neg_mean", [P, TG])
        neg_mean2 = both(sb, "neg_mean2", [P, TG])
        mean_rstd_x = both(sb, "mean_rstd_x", [P, TG])
        var_eps = both(sb, "var_eps", [P, TG])
        rstd = both(sb, "rstd", [P, TG])
        z = both(sb, "z", [P, TG, D])
        zT = both(sb, "zT", [P, R])
        k_max = both(sb, "k_max", [P, BG])
        ke = both(sb, "ke", [P, BG, T])
        k_sum = both(sb, "k_sum", [P, BG])
        k_rec = both(sb, "k_rec", [P, BG])
        q_max = [sb(f"q_max{n}", [P, TG, HEADS[n]]) for n in range(2)]
        qe = both(sb, "qe", [P, TG, D])
        qT = both(sb, "qT", [P, R])
        compact = both(sb, "compact", [P, TG, D])
        spread = both(sb, "spread", [P, TG, BT, D])
        att = both(sb, "att", [P, BG, Q])
        att_bd = [sb(f"att_bd{n}", [P, BG, D + HEADS[n]]) for n in range(2)]
        q_rec = [sb(f"q_rec{n}", [P, TG, HEADS[n]]) for n in range(2)]
        y = both(sb, "y", [P, TG, D])
        stats2 = both(sb, "stats2", [P, TG, 6])
        mv2 = both(sb, "mv2", [P, TG, 2])
        var_eps2 = both(sb, "var_eps2", [P, TG])
        rstd2 = both(sb, "rstd2", [P, TG])
        mean_rstd = both(sb, "mean_rstd", [P, TG])
        yn = both(sb, "yn", [P, TG, D])
        fs = both(sb, "fs", [P, BG, T])
        fh = both(sb, "fh", [P, BG, T])
        th = both(sb, "th", [P, BG, T])
        gate = both(sb, "gate", [P, BG, T])

        ps = ctx.enter_context(nc.psum_tensor("ps", [P, 8, 512], F32))

        def bank(product, n):
            return ps[:, PRODUCTS[product, n][0], :]

        def tiles(product, n):
            return bank(product, n).rearrange("p (j c) -> p j c", j=TG)

        def batches(product, n):
            return bank(product, n).rearrange("p (b t) -> p b t", t=T)

        def read_out_tiles(n):
            first = PRODUCTS["read_out", n][0]
            return ps[:, first:first + 2, :].rearrange("p a (b m) -> p (a b) m", b=2)

        loaded = {k: sem(f"loaded_{k}") for k in ("cond", "w_emb", "masks", "w_out")}
        loaded_vectors, loaded_w, loaded_bias = (both(sem, f"loaded_{k}_") for k in ("vectors", "w", "bias"))
        x_loaded = sem("x_loaded")
        ident_made, heads_cut, consts_laid, consts_ready, mask_terms_ready = (
            sem(k) for k in ("ident_made", "heads_cut", "consts_laid", "consts_ready", "mask_terms_ready"))
        mask_parts_ready, kept_ready, any_kept_ready, masks_turned, cond_tanh_ready = (
            sem(k) for k in ("mask_parts_ready", "kept_ready", "any_kept_ready", "masks_turned", "cond_tanh_ready"))
        cond_s_ready, cond_turned, condT_ready, w_out_ready, film_product_ready = (
            sem(k) for k in ("cond_s_ready", "cond_turned", "condT_ready", "w_out_ready", "film_product_ready"))
        film_taken, film_ready = (
            sem(k) for k in ("film_taken", "film_ready"))
        spread_zeroed, att_bd_zeroed, heads_laid, keep_ready, vectors_turned = (
            both(sem, f"{k}_") for k in ("spread_zeroed", "att_bd_zeroed", "heads_laid", "keep_ready", "vectors_turned"))
        vcol_ready, lnb_cols_ready, lnb_product_ready, b_bf_ones, bias_steps = (
            both(sem, f"{k}_") for k in ("vcol_ready", "lnb_cols_ready", "lnb_product_ready", "b_bf_ones", "bias_steps"))
        b_bf_ready, w_in_ready, neg_row_ones, neg_row_loaded = (
            both(sem, f"{k}_") for k in ("b_bf_ready", "w_in_ready", "neg_row_ones", "neg_row_loaded"))
        names = ("x_seen", "stat", "stat_seen", "stat2_seen", "moments", "var_eps", "rstd", "mean_rstd_x", "z", "z_ps",
                 "zT", "k_ps", "q_ps", "v_ps", "k_max", "k_sub",
                 "k_exp", "k_sum", "k_rec", "k_norm", "kT_ps", "q_max", "q_sub", "q_exp", "qT_ps", "qT", "compact",
                 "spread", "att_ps", "att", "att_seen", "att_bd", "y_ps", "q_rec", "y", "stat2", "moments2", "var_eps2", "rstd2",
                 "mean_rstd", "yn", "ynT_ps", "fs", "fh", "tanh", "gate", "out_ps", "done")
        S = {k: both(sem, f"s_{k}_") for k in names}
        stored = sem("stored")

        def seen(eng, name, n, g, per=1):
            eng.wait_ge(S[name][n], (g + 1) * per)

        def reused(eng, name, n, g, per=1):
            if not isinstance(g, int) or g > 0:
                eng.wait_ge(S[name][n], g * per)

        def first_group(g):
            return isinstance(g, int) and g == 0

        def run(eng, steps, order, setup):
            assert all(i < LOOPS[0][0] for i, _ in setup)

            def peeled(i):
                for name, n, lag in order:
                    if 0 <= i - lag < NG:
                        steps[name](n, i - lag)
                        if n == 0 and (i, name) in setup:
                            setup.pop((i, name))()

            done = 0
            for n, (first, last) in enumerate(LOOPS):
                for i in range(done, first):
                    peeled(i)
                with eng.Fori(first, last) as i:
                    for name, m, lag in order:
                        if m == n:
                            steps[name](n, i - lag)
                done = last
            for i in range(done, NG + max(lag for _, _, lag in LAGS)):
                peeled(i)
            assert not setup

        def per_head(ap, n):
            return ap.rearrange("p t (h c) -> p t h c", h=HEADS[n])

        def load_layer(eng, n):
            for row, v in ((LNW, "ln_w"), (LNB, "ln_b"), (BSCALE, "b_emb"), (LN2W, "ln2_w"), (LN2B, "ln2_b")):
                rows = 2 if v == "b_emb" else 1
                eng.dma_start(vectors[n][row:row + rows, :], layers[n][v].rearrange("(a c) -> a c", a=rows)
                              ).then_inc(loaded_vectors[n], 16)
            for m, v in enumerate(("Wq", "Wv", "Wk")):
                eng.dma_start(w_raw[n][:, m * D:(m + 1) * D], layers[n][v]).then_inc(loaded_w[n], 16)
            for m, v in enumerate(("bq", "bv", "bk", "b_out")):
                eng.dma_start(bias[n][:, m * D:(m + 1) * D], layers[n][v].rearrange("(a c) -> a c", a=1).to_broadcast([PARTS, D])
                              ).then_inc(loaded_bias[n], 16)

        block = ctx.enter_context(nc.Block())

        x_v = x.rearrange("b t c -> (b t) c").rearrange("(j p) c -> p j c", p=P)
        out_v = out.rearrange("b t c -> (b t) c").rearrange("(j p) c -> p j c", p=P)

        @block.sync
        def _(sp):
            def load_x(g):
                if not first_group(g):
                    sp.wait_ge(x_loaded, g * 16)
                sp.dma_start(xs[:, bass.ds(g * TG, TG), :], x_v[:, bass.ds(g * TG, TG), :]).then_inc(x_loaded, 16)

            load_x(0)
            load_layer(sp, 0)
            load_x(1)
            sp.wait_ge(mask_parts_ready, 4)
            sp.wait_ge(neg_row_ones[0], 1)
            for i in range(PARTS):
                sp.dma_start(neg_row[0][PARTS + i:PARTS + i + 1, :].rearrange("a (j p) -> a j p", p=P),
                             neg_part[:, i:i + 1, :].rearrange("j a p -> j (a p)")).then_inc(neg_row_loaded[0], 16)
            for n in range(2):
                sp.dma_start(w_emb[n][:, :, :], layers[n]["W_emb"].rearrange("(k p) m -> p k m", p=P)
                             ).then_inc(loaded["w_emb"], 16)
            for n in range(2):
                sp.dma_start(w_out[n][:, :], layers[n]["W_out"]).then_inc(loaded["w_out"], 16)
            load_layer(sp, 1)
            with sp.Fori(2, NG) as g:
                load_x(g)
            sp.wait_ge(neg_row_ones[1], 1)
            sp.dma_start(neg_row[1][PARTS:PARTS + 1, :].rearrange("a (j p) -> a j p", p=P), neg_masked[:, :]
                         ).then_inc(neg_row_loaded[1], 16)
            with sp.Fori(0, NG) as g:
                seen(sp, "done", 1, g)
                sp.dma_start(out_v[:, bass.ds(g * TG, TG), :], xs[:, bass.ds(g * TG, TG), :]).then_inc(stored, 16)
            sp.wait_ge(stored, NG * 16)

        @block.gpsimd
        def _(pool):
            g_ = nc.gpsimd
            pool.dma_start(maskf_sb[:, :], mask_f.rearrange("b t a -> (b t a)").rearrange("(j p) -> j p", p=P)
                           ).then_inc(loaded["masks"], 16)
            pool.dma_start(maski_sb[:, :], mask_i.rearrange("b t -> (b t)").rearrange("(j p) -> j p", p=P)
                           ).then_inc(loaded["masks"], 16)
            pool.dma_start(cond_sb[:, :], cond).then_inc(loaded["cond"], 16)
            g_.memset(ident[:, :], 0.0).then_inc(consts_laid, 1)
            g_.memset(exponent[:, :], -0.5).then_inc(consts_laid, 1)
            for n in range(2):
                g_.memset(head_of[n][:, :], 1.0).then_inc(consts_laid, 1)
            pool.wait_ge(consts_laid, 4)
            g_.affine_select(out=ident[:, :], in_=ident[:, :], compare_op=ALU.not_equal, fill=1.0, base=0,
                             pattern=[[-1, P]], channel_multiplier=1).then_inc(ident_made, 1)
            for n in range(2):
                w = D // HEADS[n]
                g_.affine_select(out=head_of[n][:, :], in_=head_of[n][:, :], compare_op=ALU.is_ge, fill=0.0, base=0,
                                 pattern=[[-w, HEADS[n]]], channel_multiplier=1).then_inc(heads_cut, 1)
            for n in range(2):
                w = D // HEADS[n]
                pool.wait_ge(heads_cut, n + 2)
                g_.affine_select(out=head_of[n][:, :], in_=head_of[n][:, :], compare_op=ALU.is_ge, fill=0.0,
                                 base=w - 1, pattern=[[w, HEADS[n]]], channel_multiplier=-1).then_inc(heads_cut, 1)
            def rstd_x(n, g):
                seen(pool, "var_eps", n, g, 2)
                reused(pool, "z", n, g, TG)
                g_.tensor_tensor(rstd[n][:, :], var_eps[n][:, :], exponent[:, :], ALU.pow).then_inc(S["rstd"][n], 1)
                seen(pool, "rstd", n, g)
                g_.tensor_tensor(mean_rstd_x[n][:, :], neg_mean[n][:, :], rstd[n][:, :], ALU.mult
                                 ).then_inc(S["mean_rstd_x"][n], 1)
                seen(pool, "mean_rstd_x", n, g)

            def scale_k(n, g):
                seen(pool, "k_rec", n, g)
                g_.tensor_tensor(ke[n][:, :, :], ke[n][:, :, :], k_rec[n][:, :].unsqueeze(2).to_broadcast([P, BG, T]),
                                 ALU.mult).then_inc(S["k_norm"][n], 1)
                seen(pool, "k_norm", n, g)

            def spread_att(n, g):
                reused(pool, "y_ps", n, g)
                if first_group(g):
                    pool.wait_ge(att_bd_zeroed[n], 1)
                seen(pool, "att", n, g)
                pool.sem_inc(S["att_seen"][n], 1)
                for r in range(NQ):
                    part = slice(r * Q, (r + 1) * Q)
                    g_.tensor_scalar(att_bd[n][part, :, r * Q:(r + 1) * Q], att[n][part, :, :], 1.0, 0.0,
                                     ALU.mult, ALU.add).then_inc(S["att_bd"][n], 1)
                seen(pool, "att_bd", n, g, NQ)

            def rstd_y(n, g):
                seen(pool, "var_eps2", n, g, 2)
                reused(pool, "yn", n, g, TG)
                g_.tensor_tensor(rstd2[n][:, :], var_eps2[n][:, :], exponent[:, :], ALU.pow).then_inc(S["rstd2"][n], 1)
                seen(pool, "rstd2", n, g)
                g_.tensor_tensor(mean_rstd[n][:, :], neg_mean2[n][:, :], rstd2[n][:, :], ALU.mult
                                 ).then_inc(S["mean_rstd"][n], 1)
                seen(pool, "mean_rstd", n, g)

            def film_add(n, g):
                reused(pool, "gate", n, g)
                seen(pool, "fs", n, g)
                if first_group(g):
                    pool.wait_ge(film_ready, 4)
                g_.tensor_tensor(fh[n][:, :, :], fs[n][:, :, :],
                                 film_shift[n][:, bass.ds(g * BG, BG)].unsqueeze(2).to_broadcast([P, BG, T]),
                                 ALU.add).then_inc(S["fh"][n], 1)
                seen(pool, "fh", n, g)

            def lay_ones(n):
                g_.memset(neg_row[n][0:KP[n], :].bitcast(F32), TWO_ONES).then_inc(neg_row_ones[n], 1)
                pool.wait_ge(neg_row_ones[n], 1)

            def lay_spread(n):
                g_.memset(spread[n][:, :, :, :], 0.0).then_inc(spread_zeroed[n], 1)

            def lay_att_bd(n):
                g_.memset(att_bd[n][:, :, 0:D], 0.0).then_inc(att_bd_zeroed[n], 1)
                pool.wait_ge(att_bd_zeroed[n], 1)

            def lay_first():
                lay_ones(0)
                lay_spread(0)
                lay_att_bd(0)

            run(pool, {"rstd_x": rstd_x, "scale_k": scale_k, "spread_att": spread_att, "rstd_y": rstd_y,
                       "film_add": film_add}, ORDER["pool"], 
                {(0, "rstd_x"): lay_first, (1, "scale_k"): lambda: lay_spread(1), (2, "scale_k"): lambda: lay_att_bd(1),
                 (3, "scale_k"): lambda: lay_ones(1)})

        @block.scalar
        def _(act):
            a_ = nc.scalar
            act.wait_ge(loaded["cond"], 16)
            a_.activation(cond_t[:, :], cond_sb[:, :], ACT.Tanh, scale=0.5).then_inc(cond_tanh_ready, 1)

            def normalise_x(n, g):
                reused(act, "z_ps", n, g)
                seen(act, "mean_rstd_x", n, g)
                seen(act, "rstd", n, g)
                if n == 0:
                    act.wait_ge(x_loaded, (g + 1) * 16)
                else:
                    seen(act, "done", 0, g)
                for j in range(TG):
                    a_.activation(z[n][:, j, :], xs[:, bass.ds(g * TG + j, 1), :].rearrange("p a c -> p (a c)"),
                                  ACT.Identity, scale=rstd[n][:, j:j + 1], bias=mean_rstd_x[n][:, j:j + 1]
                                  ).then_inc(S["z"][n], 1)

            def copy_zT(n, g):
                for product in ("k_ps", "q_ps", "v_ps"):
                    reused(act, product, n, g)
                seen(act, "z_ps", n, g)
                a_.copy(zT[n][:, :], bank("z_transpose", n)).then_inc(S["zT"][n], 1)

            def exp_k(n, g):
                seen(act, "k_sub", n, g)
                a_.activation(ke[n][:, :, :], ke[n][:, :, :], ACT.Exp).then_inc(S["k_exp"][n], 1)

            def exp_q(n, g):
                seen(act, "q_sub", n, g)
                a_.activation(qe[n][:, :, :], qe[n][:, :, :], ACT.Exp).then_inc(S["q_exp"][n], 1)

            def copy_v(n, g):
                reused(act, "att_ps", n, g)
                seen(act, "v_ps", n, g)
                if first_group(g):
                    act.wait_ge(spread_zeroed[0], 1)
                    act.wait_ge(keep_ready[n], 1)
                v = tiles("project_v", n)
                if n == 0:
                    for r in range(NQ):
                        part = slice(r * Q, (r + 1) * Q)
                        a_.copy(spread[0][part, :, r, :], v[part, :, :]).then_inc(S["spread"][0], 1)
                else:
                    for j in range(TG):
                        a_.activation(compact[1][:, j, :], v[:, j, :], ACT.Copy,
                                      scale=keep[1][:, bass.ds(g * TG + j, 1)]).then_inc(S["compact"][1], 1)

            def copy_k(n, g):
                reused(act, "att_ps", n, g)
                seen(act, "kT_ps", n, g)
                if first_group(g):
                    act.wait_ge(spread_zeroed[n], 1)
                    act.wait_ge(keep_ready[n], 1)
                k = tiles("k_transpose", n)
                if n == 0:
                    for j in range(TG):
                        a_.activation(compact[0][:, j, :], k[:, j, :], ACT.Copy,
                                      scale=keep[0][:, bass.ds(g * TG + j, 1)]).then_inc(S["compact"][0], 1)
                else:
                    for r in range(NQ):
                        part = slice(r * Q, (r + 1) * Q)
                        a_.copy(spread[1][part, :, r, :], k[part, :, :]).then_inc(S["spread"][1], 1)

            def copy_qT(n, g):
                reused(act, "y_ps", n, g)
                seen(act, "qT_ps", n, g)
                a_.copy(qT[n][:, :], bank("q_transpose", n)).then_inc(S["qT"][n], 1)

            def normalise_y(n, g):
                reused(act, "ynT_ps", n, g)
                seen(act, "mean_rstd", n, g)
                seen(act, "rstd2", n, g)
                seen(act, "y", n, g)
                for j in range(TG):
                    a_.activation(yn[n][:, j, :], y[n][:, j, :], ACT.Identity, scale=rstd2[n][:, j:j + 1],
                                  bias=mean_rstd[n][:, j:j + 1]).then_inc(S["yn"][n], 1)

            def tanh_h(n, g):
                reused(act, "gate", n, g)
                seen(act, "fh", n, g)
                a_.activation(th[n][:, :, :], fh[n][:, :, :], ACT.Tanh, scale=0.5).then_inc(S["tanh"][n], 1)

            run(act, {"normalise_x": normalise_x, "copy_zT": copy_zT, "copy_v": copy_v, "exp_k": exp_k, "exp_q": exp_q,
                      "copy_qT": copy_qT, "copy_k": copy_k, "normalise_y": normalise_y, "tanh_h": tanh_h},
                ORDER["scalar"], {})

        @block.vector
        def _(dve):
            v_ = nc.vector
            v_.memset(ones3[:, :], 1.0).then_inc(consts_ready, 1)
            v_.memset(ones_tiles[:, :], 1.0).then_inc(consts_ready, 1)

            def x_bn(n, g):
                reused(dve, "moments", n, g, TG)
                if n == 0:
                    dve.wait_ge(x_loaded, (g + 1) * 16)
                else:
                    seen(dve, "done", 0, g)
                dve.sem_inc(S["x_seen"][n], 1)
                for j in range(TG):
                    v_.bn_stats(stats[n][:, j, :], xs[:, bass.ds(g * TG + j, 1), :].rearrange("p a c -> p (a c)")
                                ).then_inc(S["stat"][n], 1)

            def x_aggr(n, g):
                reused(dve, "var_eps", n, g, 2)
                seen(dve, "stat", n, g, TG)
                dve.sem_inc(S["stat_seen"][n], 1)
                for j in range(TG):
                    v_.bn_aggr(mv[n][:, j, :], stats[n][:, j, :]).then_inc(S["moments"][n], 1)

            def x_eps(n, g):
                reused(dve, "mean_rstd_x", n, g)
                seen(dve, "moments", n, g, TG)
                v_.tensor_scalar(neg_mean[n][:, :], mv[n][:, :, 0], -1.0, None, ALU.mult).then_inc(S["var_eps"][n], 1)
                v_.tensor_scalar(var_eps[n][:, :], mv[n][:, :, 1], EPS, None, ALU.add).then_inc(S["var_eps"][n], 1)

            def k_maximum(n, g):
                reused(dve, "k_sub", n, g)
                seen(dve, "k_ps", n, g)
                v_.tensor_reduce(k_max[n][:, :], batches("project_k", n), X, ALU.max).then_inc(S["k_max"][n], 1)

            def k_subtract(n, g):
                seen(dve, "k_max", n, g)
                reused(dve, "kT_ps", n, g)
                v_.tensor_tensor(ke[n][:, :, :], batches("project_k", n),
                                 k_max[n][:, :].unsqueeze(2).to_broadcast([P, BG, T]), ALU.subtract
                                 ).then_inc(S["k_sub"][n], 1)

            def q_maximum(n, g):
                reused(dve, "q_sub", n, g)
                seen(dve, "q_ps", n, g)
                v_.tensor_reduce(q_max[n][:, :, :], per_head(tiles("project_q", n), n), X, ALU.max
                                 ).then_inc(S["q_max"][n], 1)

            def q_subtract(n, g):
                seen(dve, "q_max", n, g)
                reused(dve, "qT_ps", n, g)
                v_.tensor_tensor(per_head(qe[n][:, :, :], n), per_head(tiles("project_q", n), n),
                                 q_max[n][:, :, :].unsqueeze(3).to_broadcast([P, TG, HEADS[n], D // HEADS[n]]),
                                 ALU.subtract).then_inc(S["q_sub"][n], 1)

            def k_summed(n, g):
                reused(dve, "k_rec", n, g)
                seen(dve, "k_exp", n, g)
                v_.tensor_reduce(k_sum[n][:, :], ke[n][:, :, :], X, ALU.add).then_inc(S["k_sum"][n], 1)

            def k_reciprocal(n, g):
                reused(dve, "k_norm", n, g)
                seen(dve, "k_sum", n, g)
                v_.reciprocal(k_rec[n][:, :], k_sum[n][:, :]).then_inc(S["k_rec"][n], 1)

            def mask_att(n, g):
                reused(dve, "att_bd", n, g, NQ)
                seen(dve, "att_ps", n, g)
                if first_group(g):
                    dve.wait_ge(heads_laid[n], NQ + 1)
                v_.tensor_tensor(att[n][:, :, :], batches("attend", n),
                                 head_mask[n][:, :].unsqueeze(1).to_broadcast([P, BG, Q]), ALU.mult
                                 ).then_inc(S["att"][n], 1)

            def q_reciprocal(n, g):
                reused(dve, "y", n, g)
                seen(dve, "y_ps", n, g)
                v_.reciprocal(q_rec[n][:, :, :], read_out_tiles(n)[:, :, D:D + HEADS[n]]).then_inc(S["q_rec"][n], 1)

            def y_multiply(n, g):
                reused(dve, "yn", n, g, TG)
                reused(dve, "stat2", n, g, TG)
                seen(dve, "q_rec", n, g)
                v_.tensor_tensor(per_head(y[n][:, :, :], n), per_head(read_out_tiles(n)[:, :, 0:D], n),
                                 q_rec[n][:, :, :].unsqueeze(3).to_broadcast([P, TG, HEADS[n], D // HEADS[n]]),
                                 ALU.mult).then_inc(S["y"][n], 1)

            def y_bn(n, g):
                reused(dve, "moments2", n, g, TG)
                seen(dve, "y", n, g)
                for j in range(TG):
                    v_.bn_stats(stats2[n][:, j, :], y[n][:, j, :]).then_inc(S["stat2"][n], 1)

            def y_aggr(n, g):
                reused(dve, "var_eps2", n, g, 2)
                seen(dve, "stat2", n, g, TG)
                dve.sem_inc(S["stat2_seen"][n], 1)
                for j in range(TG):
                    v_.bn_aggr(mv2[n][:, j, :], stats2[n][:, j, :]).then_inc(S["moments2"][n], 1)

            def y_eps(n, g):
                reused(dve, "mean_rstd", n, g)
                seen(dve, "moments2", n, g, TG)
                v_.tensor_scalar(neg_mean2[n][:, :], mv2[n][:, :, 0], -1.0, None, ALU.mult).then_inc(S["var_eps2"][n], 1)
                v_.tensor_scalar(var_eps2[n][:, :], mv2[n][:, :, 1], EPS, None, ALU.add).then_inc(S["var_eps2"][n], 1)

            def film_mul(n, g):
                reused(dve, "fh", n, g)
                seen(dve, "ynT_ps", n, g)
                if first_group(g):
                    dve.wait_ge(film_ready, 4)
                    if n == 1:
                        dve.wait_ge(any_kept_ready, 6)
                v_.tensor_tensor(fs[n][:, :, :], batches("y_transpose", n),
                                 film_scale[n][:, bass.ds(g * BG, BG)].unsqueeze(2).to_broadcast([P, BG, T]),
                                 ALU.mult).then_inc(S["fs"][n], 1)

            def gate_h(n, g):
                reused(dve, "out_ps", n, g)
                seen(dve, "tanh", n, g)
                seen(dve, "fh", n, g)
                v_.scalar_tensor_tensor(gate[n][:, :, :], th[n][:, :, :], 1.0, fh[n][:, :, :], ALU.add, ALU.mult
                                        ).then_inc(S["gate"][n], 1)

            def residual(n, g):
                seen(dve, "out_ps", n, g)
                rows = xs[:, bass.ds(g * TG, TG), :]
                v_.tensor_tensor(rows, tiles("project_out", n), rows, ALU.add
                                 ).then_inc(S["done"][n], 1)

            def setup_columns(n):
                dve.wait_ge(vectors_turned[n], 1)
                v_.tensor_copy(vcol[n][:, :], ps[:, SETUP_BANK, 0:NVEC]).then_inc(vcol_ready[n], 1)
                dve.wait_ge(vcol_ready[n], 1)
                v_.tensor_copy(lnb_cols[n][:, :], vcol[n][:, LNB:LNB + 1].to_broadcast([P, PARTS])).then_inc(lnb_cols_ready[n], 1)

            def setup_weights(n):
                dve.wait_ge(loaded_w[n], 3 * 16)
                v_.tensor_scalar(w_in[n][:, :], w_raw[n][:, :], vcol[n][:, LNW:LNW + 1], None, ALU.mult
                                 ).then_inc(w_in_ready[n], 1)

            def setup_w_out():
                dve.wait_ge(loaded["w_out"], 2 * 16)
                for n in range(2):
                    v_.tensor_scalar(w_out[n][:, :], w_out[n][:, :], 0.5, None, ALU.mult).then_inc(w_out_ready, 1)

            def setup_masks():
                dve.wait_ge(loaded["masks"], 2 * 16)
                v_.tensor_scalar(neg_rest[:, 0, :], maskf_sb[:, :], -1.0, 1000000.0, ALU.add, ALU.mult).then_inc(mask_terms_ready, 1)
                v_.tensor_scalar(masked1[:, :], maski_sb[:, :], 1.0, None, ALU.is_equal).then_inc(mask_terms_ready, 1)
                dve.wait_ge(mask_terms_ready, 2)
                v_.tensor_scalar(kept1[:, :], masked1[:, :], -1.0, 1.0, ALU.mult, ALU.add).then_inc(kept_ready, 1)
                dve.wait_ge(kept_ready, 1)
                v_.tensor_reduce(any_kept[:, :], kept1[:, :].rearrange("j (b t) -> j b t", t=T), X, ALU.max).then_inc(any_kept_ready, 1)
                v_.tensor_scalar(neg_masked[:, :], masked1[:, :], -1e30, None, ALU.mult).then_inc(mask_parts_ready, 1)
                v_.tensor_copy(neg_part[:, 0, :], neg_rest[:, 0, :]).then_inc(mask_parts_ready, 1)
                dve.wait_ge(any_kept_ready, 1)
                v_.tensor_tensor(any_diagonal[:, :, :], ident[0:NT, 0:NT].unsqueeze(2).to_broadcast([NT, NT, BT]),
                                 any_kept[:, :].unsqueeze(1).to_broadcast([NT, NT, BT]), ALU.mult).then_inc(any_kept_ready, 1)
                for i in (1, 2):
                    dve.wait_ge(mask_parts_ready, i + 1)
                    v_.tensor_tensor(neg_rest[:, i, :], neg_rest[:, i - 1, :], neg_part[:, i - 1, :], ALU.subtract
                                     ).then_inc(mask_terms_ready, 1)
                    dve.wait_ge(mask_terms_ready, 2 + i)
                    v_.tensor_copy(neg_part[:, i, :], neg_rest[:, i, :]).then_inc(mask_parts_ready, 1)

            def setup_keep():
                dve.wait_ge(masks_turned, 1)
                for n in range(2):
                    v_.tensor_copy(keep[n][:, :], ps[:, MASK_BANK, n * NT:(n + 1) * NT]).then_inc(keep_ready[n], 1)
                v_.tensor_copy(any_batch[:, :], ps[:, MASK_BANK, 2 * NT:2 * NT + B]).then_inc(any_kept_ready, 1)

            def setup_heads(n):
                w = D // HEADS[n]
                for r in range(NQ):
                    part = slice(r * Q, (r + 1) * Q)
                    hs = head_of[n][part, r * Q // w:(r + 1) * Q // w]
                    v_.tensor_copy(head_mask[n][part, :].rearrange("p (h c) -> p h c", c=w),
                                   hs.unsqueeze(2).to_broadcast([Q, Q // w, w])).then_inc(heads_laid[n], 1)
                v_.tensor_copy(att_bd[n][:, :, D:D + HEADS[n]],
                               head_of[n][:, :].unsqueeze(1).to_broadcast([P, BG, HEADS[n]])).then_inc(heads_laid[n], 1)

            def setup_later_parts():
                dve.wait_ge(ident_made, 1)
                v_.tensor_scalar(later_parts[:, 0:1], ident[0:PARTS, 0:1], -1.0, None, ALU.add).then_inc(consts_ready, 1)
                v_.tensor_scalar(later_parts[:, 1:2], ident[0:PARTS, 2:3], -1.0, None, ALU.mult).then_inc(consts_ready, 1)

            def setup_biases(n):
                dve.wait_ge(lnb_product_ready[n], 1)
                dve.wait_ge(loaded_bias[n], 4 * 16)
                dve.wait_ge(consts_ready, 4)
                dve.wait_ge(b_bf_ones[n], 1)
                step = bias_steps[n]
                v_.tensor_tensor(bias[n][:, 0:3 * D], bias[n][:, 0:3 * D], ps[0:PARTS, SETUP_BANK, 0:3 * D], ALU.add).then_inc(step, 1)
                dve.wait_ge(step, 1)
                left = bias[n][:, :]
                for i in range(2):
                    v_.tensor_copy(b_part[n][:, i, :], left).then_inc(step, 1)
                    dve.wait_ge(step, 2 * i + 2)
                    v_.scalar_tensor_tensor(b_rest[n][:, i, :], b_part[n][:, i, :], later_parts[:, i:i + 1], left,
                                            ALU.mult, ALU.add).then_inc(step, 1)
                    dve.wait_ge(step, 2 * i + 3)
                    left = b_rest[n][:, i, :]
                v_.tensor_copy(b_bf[n][0:PARTS, :], left).then_inc(b_bf_ready[n], 1)

            def setup_silu():
                dve.wait_ge(cond_tanh_ready, 1)
                v_.scalar_tensor_tensor(cond_s[:, :], cond_t[:, :], 1.0, cond_sb[:, :], ALU.add, ALU.mult
                                        ).then_inc(cond_s_ready, 1)

            def setup_cond():
                dve.wait_ge(cond_turned, 1)
                v_.tensor_scalar(condT[:, :, :], ps[:, COND_BANK, 0:EC * B].rearrange("p (k b) -> p k b", k=EC), 0.5, None,
                                 ALU.mult).then_inc(condT_ready, 1)

            def setup_film():
                dve.wait_ge(film_product_ready, 1)
                for n in range(2):
                    col = vcol[n]
                    v_.tensor_scalar(scale1[n][:, :], ps[:, SETUP_BANK, 2 * n * B:(2 * n + 1) * B],
                                     col[:, BSCALE:BSCALE + 1], 1.0, ALU.add, ALU.add).then_inc(film_taken, 1)
                    v_.tensor_scalar(shift0[n][:, :], ps[:, SETUP_BANK, (2 * n + 1) * B:(2 * n + 2) * B],
                                     col[:, BSHIFT:BSHIFT + 1], None, ALU.add).then_inc(film_taken, 1)
                dve.wait_ge(film_taken, 4)
                for n, scale in enumerate((film_scale[0], film_plain1)):
                    col = vcol[n]
                    v_.tensor_scalar(scale[:, :], scale1[n][:, :], col[:, LN2W:LN2W + 1], None, ALU.mult
                                     ).then_inc(film_ready, 1)
                    v_.scalar_tensor_tensor(film_shift[n][:, :], scale1[n][:, :], col[:, LN2B:LN2B + 1],
                                            shift0[n][:, :], ALU.mult, ALU.add).then_inc(film_ready, 1)

            def setup_last():
                dve.wait_ge(any_kept_ready, 3)
                v_.reciprocal(any_rec[:, :], any_batch[:, :]).then_inc(any_kept_ready, 1)
                setup_heads(1)
                dve.wait_ge(any_kept_ready, 4)
                v_.tensor_tensor(one_or_nan[:, :], any_batch[:, :], any_rec[:, :], ALU.mult).then_inc(any_kept_ready, 1)
                setup_weights(1)
                dve.wait_ge(any_kept_ready, 5)
                dve.wait_ge(film_ready, 3)
                v_.tensor_tensor(film_scale[1][:, :], film_plain1[:, :], one_or_nan[:, :], ALU.mult).then_inc(any_kept_ready, 1)

            for n in range(2):
                v_.memset(b_bf[n][:, :], 1.0).then_inc(b_bf_ones[n], 1)
            def setup_first():
                setup_later_parts()
                setup_masks()
                setup_columns(0)
                setup_weights(0)
                setup_keep()
                dve.wait_ge(heads_cut, 4)
                setup_heads(0)
                setup_silu()
                setup_biases(0)
                setup_cond()

            def setup_late():
                setup_w_out()
                setup_biases(1)

            run(dve, {"x_bn": x_bn, "x_aggr": x_aggr, "x_eps": x_eps, "k_max": k_maximum, "k_sub": k_subtract,
                      "q_max": q_maximum, "q_sub": q_subtract, "k_sum": k_summed, "k_rec": k_reciprocal,
                      "mask_att": mask_att, "q_rec": q_reciprocal, "y_mul": y_multiply, "y_bn": y_bn,
                      "y_aggr": y_aggr, "y_eps": y_eps, "film_mul": film_mul, "gate_h": gate_h, "residual": residual},
                ORDER["vector"], {(0, "x_eps"): setup_first, (1, "k_sub"): lambda: setup_columns(1),
                                  (2, "q_sub"): setup_film, (3, "q_sub"): setup_late, (4, "q_sub"): setup_last})

        @block.tensor
        def _(pe):
            t_ = nc.tensor

            def transpose_rows(src, dst):
                for j in range(TG):
                    last = t_.transpose(dst[:, j * P:(j + 1) * P], src[:, j, :], ident[:, :])
                return last

            def bank_free(product, n, g):
                before = PRODUCTS[product, n][1]
                for name, m, later, per in before:
                    group = g + later
                    if isinstance(g, int):
                        group = min(group, NG - 1)
                        if group < 0:
                            continue
                    elif m != n:
                        if m == 1:
                            continue
                        group = NG - 1
                    seen(pe, name, m, group, per)

            def z_transpose(n, g):
                bank_free("z_transpose", n, g)
                seen(pe, "z", n, g, TG)
                transpose_rows(z[n], bank("z_transpose", n)).then_inc(S["z_ps"][n], 1)

            def project_k(n, g):
                if first_group(g):
                    pe.wait_ge(w_in_ready[n], 1)
                    pe.wait_ge(b_bf_ready[n], 1)
                    pe.wait_ge(neg_row_loaded[n], (KP[n] - PARTS) * 16)
                bank_free("project_k", n, g)
                seen(pe, "zT", n, g)
                t_.matmul(bank("project_k", n), w_in[n][:, 2 * D:3 * D], zT[n][:, :], start=True, stop=False)
                t_.matmul(bank("project_k", n), b_bf[n][0:KP[n], 2 * D:3 * D], neg_row[n][0:KP[n], bass.ds(g * R, R)],
                          start=False, stop=True).then_inc(S["k_ps"][n], 1)

            def project_rows(product, n, m):
                t_.matmul(bank(product, n), ones3[:, :],
                          b_bf[n][0:PARTS, m * D:(m + 1) * D].unsqueeze(1).to_broadcast([PARTS, TG, D]), start=True, stop=False)
                for j in range(TG):
                    last = t_.matmul(bank(product, n)[:, j * D:(j + 1) * D], zT[n][:, j * P:(j + 1) * P],
                                     w_in[n][:, m * D:(m + 1) * D], start=False, stop=j == TG - 1)
                return last

            def project_q(n, g):
                bank_free("project_q", n, g)
                if first_group(g):
                    pe.wait_ge(w_in_ready[n], 1)
                    pe.wait_ge(b_bf_ready[n], 1)
                seen(pe, "zT", n, g)
                project_rows("project_q", n, 0).then_inc(S["q_ps"][n], 1)

            def project_v(n, g):
                bank_free("project_v", n, g)
                if first_group(g):
                    pe.wait_ge(w_in_ready[n], 1)
                    pe.wait_ge(b_bf_ready[n], 1)
                seen(pe, "zT", n, g)
                project_rows("project_v", n, 1).then_inc(S["v_ps"][n], 1)

            def k_transpose(n, g):
                bank_free("k_transpose", n, g)
                seen(pe, "k_norm", n, g)
                transpose_rows(ke[n][:, :, :].rearrange("p (j b) t -> p j (b t)", j=TG), bank("k_transpose", n)
                               ).then_inc(S["kT_ps"][n], 1)

            def q_transpose(n, g):
                bank_free("q_transpose", n, g)
                seen(pe, "q_exp", n, g)
                transpose_rows(qe[n], bank("q_transpose", n)).then_inc(S["qT_ps"][n], 1)

            def attend(n, g):
                bank_free("attend", n, g)
                seen(pe, "compact", n, g, TG)
                seen(pe, "spread", n, g, NQ)
                for j in range(TG):
                    for r in range(NQ):
                        last = t_.matmul(ps[r * Q:(r + 1) * Q, PRODUCTS["attend", n][0], j * P:(j + 1) * P],
                                         compact[n][:, j, r * Q:(r + 1) * Q], spread[n][:, j, :, r * Q:(r + 1) * Q],
                                         start=True, stop=True, tile_position=(0, r * Q))
                last.then_inc(S["att_ps"][n], 1)

            def read_out(n, g):
                bank_free("read_out", n, g)
                if first_group(g):
                    pe.wait_ge(heads_laid[n], NQ + 1)
                wide = read_out_tiles(n)
                seen(pe, "att_bd", n, g, NQ)
                seen(pe, "qT", n, g)
                for b in range(BG):
                    j, r = b // BT, b % BT
                    last = t_.matmul(wide[r * T:(r + 1) * T, j, 0:D + HEADS[n]], qT[n][:, b * T:(b + 1) * T],
                                     att_bd[n][:, b, :], start=True, stop=True, tile_position=(0, r * T))
                last.then_inc(S["y_ps"][n], 1)

            def y_transpose(n, g):
                bank_free("y_transpose", n, g)
                seen(pe, "yn", n, g, TG)
                transpose_rows(yn[n], bank("y_transpose", n)).then_inc(S["ynT_ps"][n], 1)

            def project_out(n, g):
                bank_free("project_out", n, g)
                if first_group(g):
                    pe.wait_ge(w_out_ready, 2)
                seen(pe, "gate", n, g)
                h = gate[n][:, :, :].rearrange("p (j b) t -> p j (b t)", j=TG)
                t_.matmul(bank("project_out", n), ones3[:, :],
                          b_bf[n][0:PARTS, 3 * D:4 * D].unsqueeze(1).to_broadcast([PARTS, TG, D]), start=True, stop=False)
                for j in range(TG):
                    last = t_.matmul(bank("project_out", n)[:, j * P:(j + 1) * P], h[:, j, :], w_out[n][:, :], start=False,
                                     stop=j == TG - 1)
                last.then_inc(S["out_ps"][n], 1)

            def vector_columns(n):
                pe.wait_ge(loaded_vectors[n], 5 * 16)
                t_.transpose(ps[:, SETUP_BANK, 0:NVEC], vectors[n][:, :], ident[0:NVEC, 0:NVEC]).then_inc(vectors_turned[n], 1)

            def bias_rows(n):
                pe.wait_ge(lnb_cols_ready[n], 1)
                pe.wait_ge(loaded_w[n], 3 * 16)
                t_.matmul(ps[0:PARTS, SETUP_BANK, 0:3 * D], lnb_cols[n][:, :], w_raw[n][:, :], start=True, stop=True
                          ).then_inc(lnb_product_ready[n], 1)

            pe.wait_ge(ident_made, 1)
            vector_columns(0)
            pe.wait_ge(loaded["masks"], 2 * 16)
            pe.wait_ge(kept_ready, 1)
            t_.transpose(ps[:, MASK_BANK, 0:NT], maskf_sb[:, :], ident[0:NT, 0:NT])
            t_.transpose(ps[:, MASK_BANK, NT:2 * NT], kept1[:, :], ident[0:NT, 0:NT])
            pe.wait_ge(any_kept_ready, 2)
            pe.wait_ge(consts_ready, 2)
            t_.matmul(ps[:, MASK_BANK, 2 * NT:2 * NT + B], ones_tiles[:, :], any_diagonal[:, :, :].rearrange("j i b -> j (i b)"),
                      start=True, stop=True).then_inc(masks_turned, 1)
            bias_rows(0)

            def transpose_cond():
                pe.wait_ge(cond_s_ready, 1)
                for k in range(EC):
                    last = t_.transpose(ps[:, COND_BANK, k * B:(k + 1) * B], cond_s[:, k * P:(k + 1) * P], ident[:, :])
                last.then_inc(cond_turned, 1)

            def columns_1():
                pe.wait_ge(bias_steps[0], 1)
                vector_columns(1)
                pe.wait_ge(any_kept_ready, 3)
                pe.wait_ge(condT_ready, 1)

            def film_products():
                pe.wait_ge(vcol_ready[1], 1)
                pe.wait_ge(loaded["w_emb"], 2 * 16)
                for n in range(2):
                    for half in range(2):
                        for k in range(EC):
                            last = t_.matmul(ps[:, SETUP_BANK, (2 * n + half) * B:(2 * n + half + 1) * B],
                                             w_emb[n][:, k, half * D:(half + 1) * D], condT[:, k, :],
                                             start=(k == 0), stop=(k == EC - 1))
                last.then_inc(film_product_ready, 1)

            def bias_rows_1():
                pe.wait_ge(film_taken, 4)
                bias_rows(1)

            def leave_bank():
                pe.wait_ge(bias_steps[1], 1)

            run(pe, {"z_transpose": z_transpose, "project_k": project_k, "project_q": project_q,
                     "project_v": project_v, "q_transpose": q_transpose, "k_transpose": k_transpose,
                     "attend": attend, "read_out": read_out, "y_transpose": y_transpose,
                     "project_out": project_out}, ORDER["tensor"],
                {(0, "z_transpose"): transpose_cond, (0, "project_v"): columns_1, (1, "project_v"): film_products,
                 (2, "project_v"): bias_rows_1, (3, "project_v"): leave_bank})


_L0 = {"ln_w": "L0_cond_ln_w", "ln_b": "L0_cond_ln_b", "Wq": "L0_cond_Wq", "bq": "L0_cond_bq", "Wk": "L0_cond_Wk",
       "bk": "L0_cond_bk", "Wv": "L0_cond_Wv", "bv": "L0_cond_bv", "W_emb": "L0_cond_W_emb", "b_emb": "L0_cond_b_emb",
       "ln2_w": "L0_cond_ln2_w", "ln2_b": "L0_cond_ln2_b", "W_out": "L0_cond_W_out", "b_out": "L0_cond_b_out"}
_L1 = {"ln_w": "L1_cond_norm_scale", "ln_b": "L1_cond_norm_bias", "Wq": "L1_cond_Wq", "bq": "L1_cond_bq",
       "Wk": "L1_cond_Wk", "bk": "L1_cond_bk", "Wv": "L1_cond_Wv", "bv": "L1_cond_bv", "W_emb": "L1_cond_film_emb_W",
       "b_emb": "L1_cond_film_emb_b", "ln2_w": "L1_cond_film_norm_scale", "ln2_b": "L1_cond_film_norm_bias",
       "W_out": "L1_cond_film_out_W", "b_out": "L1_cond_film_out_b"}


def kernel(**inputs):
    import numpy as np
    import concourse.bacc as bacc
    from concourse.bass_utils import run_bass_kernel_spmd

    nc = bacc.Bacc("TRN2", target_bir_lowering=False, num_devices=1)
    arrays, aps = {}, {}
    for name in ["x", "cond_2048", "mask_BxSx1_fk1", "mask_BxS_ik0", *_L0.values(), *_L1.values()]:
        a = np.ascontiguousarray(inputs[name])
        arrays[f"in_{name}"] = a
        aps[name] = nc.dram_tensor(f"in_{name}", a.shape, mybir.dt.from_np(a.dtype), kind="ExternalInput").ap()
    out = nc.dram_tensor("out_0", (B, T, D), F32, kind="ExternalOutput").ap()
    layers = [{k: aps[v] for k, v in names.items()} for names in (_L0, _L1)]
    build(nc, aps["x"], aps["cond_2048"], aps["mask_BxSx1_fk1"], aps["mask_BxS_ik0"], layers, out)
    r = run_bass_kernel_spmd(nc, [arrays], core_ids=[0])
    return r.results[0]["out_0"]
```
